# Optimizing a Trainium2 kernel written in Bass

```python
import numpy as np
import jax
import jax.numpy as jnp

def _softmax(x, axis=-1):
    return jax.nn.softmax(x, axis=axis)

def _gelu(x):
    return jax.nn.gelu(x, approximate=True)

def _silu(x):
    return jax.nn.silu(x)

def _sigmoid(x):
    return jax.nn.sigmoid(x)

def _layernorm(x, axis=-1, eps=1e-05):
    m = jnp.mean(x, axis=axis, keepdims=True)
    v = jnp.var(x, axis=axis, keepdims=True)
    return (x - m) / jnp.sqrt(v + eps)

def _scatter_add(tgt, idx, src, axis=0):
    return tgt.at[idx].add(src)

def _segment_sum(src, seg, n):
    return jax.ops.segment_sum(src, seg, n)
kernel_name = 'mk_dlrm_tower_d1_rec_r8_d764be'

def setup_inputs(seed: int=0):
    np.random.seed(seed)
    _w = jnp.asarray

    def _rec_inputs():
        import jax
        import jax.numpy as jnp
        _tk = jax.random.key(seed)
        ids = jnp.stack([jax.random.randint(jax.random.fold_in(_tk, 200 + f), (512,), 0, v, jnp.int32) for f, v in enumerate([1250, 1250, 1250, 12500, 12500, 1250, 1250, 12500, 1250, 12500, 12500, 125000, 1250, 12500, 1250, 1250, 12500, 12500, 1000, 1250, 1000, 1000, 1000, 1000, 1250, 1000])], axis=1)
        tbl_0 = 0.05 * jax.random.normal(jax.random.fold_in(_tk, 500 + 0), (1250, 128), jnp.float32)
        tbl_1 = 0.05 * jax.random.normal(jax.random.fold_in(_tk, 500 + 1), (1250, 128), jnp.float32)
        tbl_2 = 0.05 * jax.random.normal(jax.random.fold_in(_tk, 500 + 2), (1250, 128), jnp.float32)
        tbl_3 = 0.05 * jax.random.normal(jax.random.fold_in(_tk, 500 + 3), (12500, 128), jnp.float32)
        tbl_4 = 0.05 * jax.random.normal(jax.random.fold_in(_tk, 500 + 4), (12500, 128), jnp.float32)
        tbl_5 = 0.05 * jax.random.normal(jax.random.fold_in(_tk, 500 + 5), (1250, 128), jnp.float32)
        tbl_6 = 0.05 * jax.random.normal(jax.random.fold_in(_tk, 500 + 6), (1250, 128), jnp.float32)
        tbl_7 = 0.05 * jax.random.normal(jax.random.fold_in(_tk, 500 + 7), (12500, 128), jnp.float32)
        tbl_8 = 0.05 * jax.random.normal(jax.random.fold_in(_tk, 500 + 8), (1250, 128), jnp.float32)
        tbl_9 = 0.05 * jax.random.normal(jax.random.fold_in(_tk, 500 + 9), (12500, 128), jnp.float32)
        tbl_10 = 0.05 * jax.random.normal(jax.random.fold_in(_tk, 500 + 10), (12500, 128), jnp.float32)
        tbl_11 = 0.05 * jax.random.normal(jax.random.fold_in(_tk, 500 + 11), (125000, 128), jnp.float32)
        tbl_12 = 0.05 * jax.random.normal(jax.random.fold_in(_tk, 500 + 12), (1250, 128), jnp.float32)
        tbl_13 = 0.05 * jax.random.normal(jax.random.fold_in(_tk, 500 + 13), (12500, 128), jnp.float32)
        tbl_14 = 0.05 * jax.random.normal(jax.random.fold_in(_tk, 500 + 14), (1250, 128), jnp.float32)
        tbl_15 = 0.05 * jax.random.normal(jax.random.fold_in(_tk, 500 + 15), (1250, 128), jnp.float32)
        tbl_16 = 0.05 * jax.random.normal(jax.random.fold_in(_tk, 500 + 16), (12500, 128), jnp.float32)
        tbl_17 = 0.05 * jax.random.normal(jax.random.fold_in(_tk, 500 + 17), (12500, 128), jnp.float32)
        tbl_18 = 0.05 * jax.random.normal(jax.random.fold_in(_tk, 500 + 18), (1000, 128), jnp.float32)
        tbl_19 = 0.05 * jax.random.normal(jax.random.fold_in(_tk, 500 + 19), (1250, 128), jnp.float32)
        tbl_20 = 0.05 * jax.random.normal(jax.random.fold_in(_tk, 500 + 20), (1000, 128), jnp.float32)
        tbl_21 = 0.05 * jax.random.normal(jax.random.fold_in(_tk, 500 + 21), (1000, 128), jnp.float32)
        tbl_22 = 0.05 * jax.random.normal(jax.random.fold_in(_tk, 500 + 22), (1000, 128), jnp.float32)
        tbl_23 = 0.05 * jax.random.normal(jax.random.fold_in(_tk, 500 + 23), (1000, 128), jnp.float32)
        tbl_24 = 0.05 * jax.random.normal(jax.random.fold_in(_tk, 500 + 24), (1250, 128), jnp.float32)
        tbl_25 = 0.05 * jax.random.normal(jax.random.fold_in(_tk, 500 + 25), (1000, 128), jnp.float32)
        _rk = jax.random.fold_in(_tk, 7)
        r_dense_features = -0.000520686 + 1.00062 * jax.random.normal(jax.random.fold_in(_rk, 101), (512, 128), jnp.float32)
        W_top1 = 0.0405887 * jax.random.normal(jax.random.fold_in(_tk, 801), (607, 512), jnp.float32)
        W_top2 = 0.0441942 * jax.random.normal(jax.random.fold_in(_tk, 802), (512, 256), jnp.float32)
        W_top3 = 0.0625 * jax.random.normal(jax.random.fold_in(_tk, 803), (256, 1), jnp.float32)
        b_top1 = jnp.zeros((512,), jnp.float32)
        b_top2 = jnp.zeros((256,), jnp.float32)
        return (r_dense_features, ids, tbl_0, tbl_1, tbl_2, tbl_3, tbl_4, tbl_5, tbl_6, tbl_7, tbl_8, tbl_9, tbl_10, tbl_11, tbl_12, tbl_13, tbl_14, tbl_15, tbl_16, tbl_17, tbl_18, tbl_19, tbl_20, tbl_21, tbl_22, tbl_23, tbl_24, tbl_25, W_top1, b_top1, W_top2, b_top2, W_top3)
    r_dense_features, ids, tbl_0, tbl_1, tbl_2, tbl_3, tbl_4, tbl_5, tbl_6, tbl_7, tbl_8, tbl_9, tbl_10, tbl_11, tbl_12, tbl_13, tbl_14, tbl_15, tbl_16, tbl_17, tbl_18, tbl_19, tbl_20, tbl_21, tbl_22, tbl_23, tbl_24, tbl_25, W_top1, b_top1, W_top2, b_top2, W_top3 = _rec_inputs()

    def _L0_rec_setup():
        import jax, jax.numpy as jnp
        import numpy as np
        NUM_SPARSE = 26
        EMBED_DIM = 128
        BATCH = 2048
        key = jax.random.key(seed)
        k1, k2 = jax.random.split(key)
        dense_features = jax.random.normal(k1, (BATCH, EMBED_DIM), dtype=jnp.float32)
        sparse_features = jax.random.normal(k2, (BATCH, NUM_SPARSE, EMBED_DIM), dtype=jnp.float32)
        return {'dense_features': dense_features, 'sparse_features': sparse_features}
    _L0_rec_all = _L0_rec_setup()
    _L0_rec_in = {k: v for k, v in _L0_rec_all.items() if k in ()}
    del _L0_rec_all
    return {'r_dense_features': r_dense_features, 'ids': ids, 'tbl_0': tbl_0, 'tbl_1': tbl_1, 'tbl_2': tbl_2, 'tbl_3': tbl_3, 'tbl_4': tbl_4, 'tbl_5': tbl_5, 'tbl_6': tbl_6, 'tbl_7': tbl_7, 'tbl_8': tbl_8, 'tbl_9': tbl_9, 'tbl_10': tbl_10, 'tbl_11': tbl_11, 'tbl_12': tbl_12, 'tbl_13': tbl_13, 'tbl_14': tbl_14, 'tbl_15': tbl_15, 'tbl_16': tbl_16, 'tbl_17': tbl_17, 'tbl_18': tbl_18, 'tbl_19': tbl_19, 'tbl_20': tbl_20, 'tbl_21': tbl_21, 'tbl_22': tbl_22, 'tbl_23': tbl_23, 'tbl_24': tbl_24, 'tbl_25': tbl_25, 'W_top1': W_top1, 'b_top1': b_top1, 'W_top2': W_top2, 'b_top2': b_top2, 'W_top3': W_top3}

def reference(r_dense_features, ids, tbl_0, tbl_1, tbl_2, tbl_3, tbl_4, tbl_5, tbl_6, tbl_7, tbl_8, tbl_9, tbl_10, tbl_11, tbl_12, tbl_13, tbl_14, tbl_15, tbl_16, tbl_17, tbl_18, tbl_19, tbl_20, tbl_21, tbl_22, tbl_23, tbl_24, tbl_25, W_top1, b_top1, W_top2, b_top2, W_top3):
    import jax
    import jax.numpy as jnp

    def _L0_rec_ref(dense_features, sparse_features):
        import jax, jax.numpy as jnp
        import numpy as np
        NUM_SPARSE = 26
        EMBED_DIM = 128
        BATCH = 2048
        F = NUM_SPARSE + 1
        combined = jnp.concatenate([dense_features[:, None, :], sparse_features], axis=1)
        interactions = jnp.einsum('bfd,bgd->bfg', combined, combined)
        iu, ju = jnp.triu_indices(F, k=1)
        interactions_flat = interactions[:, iu, ju]
        return jnp.concatenate([dense_features, interactions_flat], axis=1)
    e = jnp.stack([tbl_0[ids[:, 0]], tbl_1[ids[:, 1]], tbl_2[ids[:, 2]], tbl_3[ids[:, 3]], tbl_4[ids[:, 4]], tbl_5[ids[:, 5]], tbl_6[ids[:, 6]], tbl_7[ids[:, 7]], tbl_8[ids[:, 8]], tbl_9[ids[:, 9]], tbl_10[ids[:, 10]], tbl_11[ids[:, 11]], tbl_12[ids[:, 12]], tbl_13[ids[:, 13]], tbl_14[ids[:, 14]], tbl_15[ids[:, 15]], tbl_16[ids[:, 16]], tbl_17[ids[:, 17]], tbl_18[ids[:, 18]], tbl_19[ids[:, 19]], tbl_20[ids[:, 20]], tbl_21[ids[:, 21]], tbl_22[ids[:, 22]], tbl_23[ids[:, 23]], tbl_24[ids[:, 24]], tbl_25[ids[:, 25]]], axis=1)
    z = _L0_rec_ref(r_dense_features, e)
    z = z.reshape(z.shape[0], -1)
    h = jnp.concatenate([z, r_dense_features], axis=1)
    h = jnp.maximum(h @ W_top1 + b_top1, 0.0)
    h = jnp.maximum(h @ W_top2 + b_top2, 0.0)
    y = h @ W_top3
    return y

_drawn_inputs = setup_inputs


def setup_inputs(seed=0):
    import zlib

    import numpy as np

    out = dict(_drawn_inputs(seed))
    spreads = {'b_top1': (0.0, 0.1), 'b_top2': (0.0, 0.1)}
    factors = {}
    for name, (base, spread) in spreads.items():
        noise = np.random.default_rng([zlib.crc32(name.encode()), seed]).standard_normal(out[name].shape)
        drawn = base * np.exp(spread * noise) if base else spread * noise
        out[name] = jnp.asarray(drawn.astype(out[name].dtype))
    for name, factor in factors.items():
        out[name] = (out[name] * factor).astype(out[name].dtype)
    return out
```

```python
import concourse.bass as bass
from concourse import mybir
from concourse.alu_op_type import AluOpType as ALU
from contextlib import ExitStack

F32 = mybir.dt.float32
F32R = mybir.dt.float32r
F16 = mybir.dt.float16
I32 = mybir.dt.int32
ACT = mybir.ActivationFunctionType

P = 128


def dlrm_program(nc, dense, ids, tables, w1, b1, w2, b2, w3, y_out):
    B, D = dense.shape
    NTAB = len(tables)
    F = NTAB + 1
    O1, O2 = w2.shape
    PAIRS = F * (F - 1) // 2
    TILES = B // P
    OC1, OC2 = O1 // P, O2 // P
    assert D == P and F == 27 and w1.shape[0] == D + PAIRS + D

    ROWS = 32
    QUADS = P // ROWS
    MOV = F - 1
    CHUNKS = MOV // QUADS
    DUP = MOV - CHUNKS * QUADS
    FIRST_MAIN = DUP + 1
    assert DUP + F <= ROWS

    ONE_HOT = list(range(18, 26))
    GATHERED = [k for k in range(NTAB) if k not in ONE_HOT]
    NOH = len(ONE_HOT)
    TP = 125
    TC = [tables[k].shape[0] // TP for k in ONE_HOT]
    TC_MAX = max(TC)
    assert all(tables[k].shape[0] == TP * c for k, c in zip(ONE_HOT, TC))
    assert all(tables[k].shape[0] <= 2048 for k in ONE_HOT)
    OH_RING = 8
    CHUNKS_BEFORE = [sum(TC[:n]) for n in range(NOH + 1)]

    GROUPS = [GATHERED[n:n + 4] for n in range(0, len(GATHERED), 4)]
    NG = len(GROUPS)

    BLOCK = 4
    BLOCKS_PER_BANK = 4
    GRAM_BANKS = 2
    GROUP_BLOCKS = BLOCKS_PER_BANK * GRAM_BANKS
    GROUP_ROWS = GROUP_BLOCKS * BLOCK
    GRAMS = P // GROUP_ROWS

    def pair_row(i, j):
        return D + i * F - i * (i + 1) // 2 + (j - i - 1)

    ctx = ExitStack()
    with ctx:
        def sb(name, shape, dt):
            return ctx.enter_context(nc.sbuf_tensor(name, shape, dt))

        def sem(name):
            return ctx.enter_context(nc.semaphore(name))

        et = sb("et", [P, B, ROWS], F32)
        xt = sb("xt", [P, B], F32)
        z = sb("z", [P, CHUNKS, B], F32)
        rows = sb("rows", [P, 2, len(GATHERED), D], F32)
        x_sb = sb("x_sb", [P, TILES, D], F32)
        ids_sb = sb("ids_sb", [P, TILES, NTAB], I32)
        ids16 = sb("ids16", [P, TILES, NOH], F16)
        ident = sb("ident", [P, P], F32)
        ident16 = sb("ident16", [P, P], F16)
        first_row = sb("first_row", [P, 2], F32)
        table_sb = sb("table_sb", [P, 3, TC_MAX, D], F32)
        table_hi = sb("table_hi", [P, 2, TC_MAX, D], F32R)
        table_lo = sb("table_lo", [P, 2, TC_MAX, D], F32R)
        offset16 = sb("offset16", [P, 2, B], F16)
        one_hot = sb("one_hot", [P, OH_RING, B], F32R)
        w1_pairs = sb("w1_pairs", [P, CHUNKS, O1], F32)
        w1_dense = sb("w1_dense", [P, 2, O1], F32)
        w1_dense_sum = sb("w1_dense_sum", [P, O1], F32)
        w2_sb = sb("w2_sb", [P, OC1, O2], F32)
        NVEC = OC1 + 2 * OC2
        vec_rows = sb("vec_rows", [NVEC, P], F32)
        vec = sb("vec", [P, NVEC], F32)
        h1 = sb("h1", [P, 2, OC1, P], F32)
        h2 = sb("h2", [P, 2, OC2, P], F32)
        y_sb = sb("y_sb", [1, B], F32)
        ps = ctx.enter_context(nc.psum_tensor("ps", [P, 8, 512], F32))

        def sum_bank(n):
            return ps[:, 2 * (n % 2), :]

        def spread_bank(n):
            return ps[:, 2 * (n % 2) + 1, :]

        def tr_bank(n):
            return ps[:, 4 + n % 2, :]

        HALF1, HALF2 = OC1 // 2, OC2 // 2

        def l1_ps(o):
            return ps[:, 6 + o // HALF1, o % HALF1 * P:(o % HALF1 + 1) * P]

        def l2_ps(o):
            at = HALF1 + o % HALF2
            return ps[:, 6 + o // HALF2, at * P:(at + 1) * P]

        l3_ps = ps[0:1, 6, (HALF1 + HALF2) * P:(HALF1 + HALF2 + 1) * P]
        vec_ps = ps[:, 7, 0:NVEC]

        ids_loaded, x_loaded, vec_loaded = sem("ids_loaded"), sem("x_loaded"), sem("vec_loaded")
        wd_loaded, w2_loaded, w1_loaded = sem("wd_loaded"), sem("w2_loaded"), sem("w1_loaded")
        table_loaded = [sem(f"table_loaded{n}") for n in range(NOH)]
        gathered = [[sem(f"gathered{t}_{g}") for g in range(NG)] for t in range(TILES)]
        y_stored = sem("y_stored")
        ident_zero, ident_ready, first_row_ready = sem("ident_zero"), sem("ident_ready"), sem("first_row_ready")
        w1_zeroed, wd_ready, et_padded = sem("w1_zeroed"), sem("wd_ready"), sem("et_padded")
        ids16_ready, ident16_ready = sem("ids16_ready"), sem("ident16_ready")
        spread_done, offset_ready = sem("spread_done"), sem("offset_ready")
        hi_ready, lo_ready = sem("hi_ready"), sem("lo_ready")
        one_hot_ready, one_hot_used = sem("one_hot_ready"), sem("one_hot_used")
        sum_moved = sem("sum_moved")
        tr_done, tr_moved_act, tr_moved_dve = sem("tr_done"), sem("tr_moved_act"), sem("tr_moved_dve")
        vec_done, vec_ready = sem("vec_done"), sem("vec_ready")
        gram_done = sem("gram_done")
        main_act, main_dve, z_act, z_dve = sem("main_act"), sem("main_dve"), sem("z_act"), sem("z_dve")
        l1_done, h1_act, h1_dve = sem("l1_done"), sem("h1_act"), sem("h1_dve")
        l2_done, h2_act, h2_dve = sem("l2_done"), sem("h2_act"), sem("h2_dve")
        l3_done, y_ready = sem("l3_done"), sem("y_ready")

        def tr_number(t, g):
            return 1 + t * NG + g

        def moved_by_act(n):
            return n // 2 + 1

        def moved_by_dve(n):
            return (n + 1) // 2

        def w1_pieces():
            for i in range(F - 1):
                skip = max(0, i + 1 - FIRST_MAIN)
                g, c = divmod(skip, CHUNKS)
                if c:
                    yield g, 1, DUP + i, c, CHUNKS - c, pair_row(i, FIRST_MAIN + skip)
                    g += 1
                if g < QUADS:
                    yield g, QUADS - g, DUP + i, 0, CHUNKS, pair_row(i, FIRST_MAIN + CHUNKS * g)
            for i in range(DUP):
                yield 0, 1, i, i, DUP - i, pair_row(i, i + 1)

        PIECES = list(w1_pieces())

        block = ctx.enter_context(nc.Block())

        @block.sync
        def _(sp):
            def load_table(n):
                if n >= 3:
                    sp.wait_ge(lo_ready, n - 2)
                src = tables[ONE_HOT[n]].rearrange("(p c) d -> p c d", p=TP)
                sp.dma_start(table_sb[0:TP, n % 3, 0:TC[n], :], src).then_inc(table_loaded[n], 16)

            def load_w1(pieces):
                for g, ng, p, c, nc_, row in pieces:
                    src = w1[row:row + ng * nc_, :].rearrange("(g c) o -> g c o", g=ng)
                    first = ROWS * g + p
                    dst = w1_pairs[first:first + ROWS * (ng - 1) + 1:ROWS, c:c + nc_, :]
                    sp.dma_start(dst, src).then_inc(w1_loaded, 16)

            sp.dma_start(ids_sb[:], ids.rearrange("(t p) k -> p t k", p=P)).then_inc(ids_loaded, 16)
            load_table(0)
            load_table(1)
            sp.dma_start(x_sb[:], dense.rearrange("(t p) d -> p t d", p=P)).then_inc(x_loaded, 16)
            load_table(2)
            sp.dma_start(vec_rows[0:OC1, :], b1.rearrange("(o p) -> o p", p=P)).then_inc(vec_loaded, 16)
            sp.dma_start(vec_rows[OC1:OC1 + OC2, :], b2.rearrange("(o p) -> o p", p=P)).then_inc(vec_loaded, 16)
            sp.dma_start(vec_rows[OC1 + OC2:NVEC, :],
                         w3.rearrange("(o p) u -> o (p u)", p=P)).then_inc(vec_loaded, 16)
            sp.wait_ge(w1_zeroed, 1)
            share = -(-len(PIECES) // (NOH - 3))
            for n in range(3, NOH):
                load_table(n)
                load_w1(PIECES[(n - 3) * share:(n - 2) * share])
            sp.dma_start(w1_dense[:, 0, :], w1[0:D, :]).then_inc(wd_loaded, 16)
            sp.dma_start(w1_dense[:, 1, :], w1[D + PAIRS:D + PAIRS + D, :]).then_inc(wd_loaded, 16)
            sp.dma_start(w2_sb[:], w2.rearrange("(k p) o -> p k o", p=P)).then_inc(w2_loaded, 16)
            sp.wait_ge(y_ready, TILES)
            sp.dma_start(y_out.rearrange("b u -> u b"), y_sb[:]).then_inc(y_stored, 16)
            sp.wait_ge(y_stored, 16)

        @block.gpsimd
        def _(pool):
            pool.memset(ident[:], 0.0).then_inc(ident_zero, 1)
            pool.wait_ge(ident_zero, 1)
            pool.affine_select(out=ident[:], in_=ident[:], compare_op=ALU.not_equal, fill=1.0, base=0,
                               pattern=[[-1, P]], channel_multiplier=1).then_inc(ident_ready, 1)
            for n, c in enumerate(sorted(set(TC))):
                pool.iota(first_row[:, n:n + 1], pattern=[[0, 1]], base=0, channel_multiplier=-c,
                          allow_small_or_imprecise_dtypes=True).then_inc(first_row_ready, 1)
            pool.wait_ge(ids_loaded, 16)
            for t in range(TILES):
                for g, group in enumerate(GROUPS):
                    if t >= 2:
                        pool.wait_ge(tr_done, tr_number(t - 2, g) + 1)
                    for k in group:
                        pool.indirect_dma_start(
                            rows[:, t % 2, GATHERED.index(k), :], None, tables[k],
                            bass.IndirectOffsetOnAxis(ids_sb[:, t, k:k + 1], 0),
                        ).then_inc(gathered[t][g], 16)

        def runs(t, g):
            features = [k + 1 for k in GROUPS[g]]
            start = 0
            for n in range(1, len(features) + 1):
                if n == len(features) or features[n] != features[n - 1] + 1:
                    yield features[start], features[n - 1] + 1, start, DUP + features[start]
                    start = n
            again = [f for f in features if f < DUP]
            if again:
                yield again[0], again[-1] + 1, features.index(again[0]), again[0]

        def move_transposed(copy, t, g):
            bank = tr_bank(tr_number(t, g))
            for f, f_end, place, col in runs(t, g):
                n = f_end - f
                last = copy(et[:, t * P:(t + 1) * P, col:col + n].rearrange("p b f -> p f b"),
                            bank[:, place * P:(place + n) * P].rearrange("p (f b) -> p f b", f=n))
            return last

        def products(gi, q, w, n):
            b = GRAM_BANKS * (gi % 2)
            width = BLOCK * MOV
            v = ps[ROWS * q:ROWS * (q + 1), b:b + GRAM_BANKS, 0:BLOCKS_PER_BANK * width]
            v = v.rearrange("p k (m w) -> p k m w", m=BLOCKS_PER_BANK)
            return v[:, :, :, MOV * q + w:MOV * q + w + n]

        def slots(gi, q, g, c, n):
            b0 = gi * GROUP_ROWS
            v = z[ROWS * g:ROWS * (g + 1), c:c + n, b0:b0 + GROUP_ROWS]
            v = v.rearrange("p c (k m q) -> p k m c q", k=GRAM_BANKS, m=BLOCKS_PER_BANK)
            return v[:, :, :, :, q]

        def move_products(eng, copy, gi, quads, main_sem, z_sem):
            for g in range(QUADS):
                for q in quads:
                    copy(slots(gi, q, g, 0, CHUNKS),
                         products(gi, q, FIRST_MAIN - 1 + CHUNKS * g, CHUNKS)).then_inc(main_sem, 1)
            eng.wait_ge(main_sem, len(quads) * (QUADS * gi + 1))
            for q in quads:
                last = copy(slots(gi, q, 0, 0, DUP)[0:DUP], products(gi, q, 0, DUP)[0:DUP])
            last.then_inc(z_sem, 1)

        @block.scalar
        def _(act):
            def copy(out, in_):
                return act.activation(out, in_, ACT.Copy)

            def high_part(n):
                act.wait_ge(table_loaded[n], 16)
                if n >= 2:
                    act.wait_ge(one_hot_used, CHUNKS_BEFORE[n - 1])
                copy(table_hi[0:TP, n % 2, 0:TC[n], :], table_sb[0:TP, n % 3, 0:TC[n], :]).then_inc(hi_ready, 1)

            def offsets(n):
                act.wait_ge(spread_done, n + 1)
                if n >= 2:
                    act.wait_ge(one_hot_ready, CHUNKS_BEFORE[n - 1])
                which = sorted(set(TC)).index(TC[n])
                act.activation(offset16[0:TP, n % 2, :], spread_bank(n)[0:TP, :], ACT.Identity,
                               bias=first_row[0:TP, which:which + 1]).then_inc(offset_ready, 1)

            def move_sum(n):
                act.wait_ge(one_hot_used, CHUNKS_BEFORE[n + 1])
                col = DUP + ONE_HOT[n] + 1
                copy(et[:, :, col], sum_bank(n)).then_inc(sum_moved, 1)

            def move_group(t, g):
                n = tr_number(t, g)
                if n % 2 == 0:
                    act.wait_ge(tr_done, n + 1)
                    move_transposed(copy, t, g).then_inc(tr_moved_act, 1)

            act.wait_ge(first_row_ready, len(set(TC)))
            offsets(0)
            high_part(0)
            offsets(1)
            high_part(1)
            act.wait_ge(tr_done, 1)
            copy(et[:, :, 0], tr_bank(0))
            copy(et[:, :, DUP], tr_bank(0))
            copy(xt[:], tr_bank(0)).then_inc(tr_moved_act, 1)
            act.wait_ge(vec_done, 1)
            copy(vec[:], vec_ps).then_inc(vec_ready, 1)
            for n in range(2, NOH):
                move_sum(n - 2)
                high_part(n)
                offsets(n)
            move_sum(NOH - 2)
            move_sum(NOH - 1)

            for g in range(NG):
                move_group(0, g)
            for t in range(TILES):
                for gi in range(GRAMS * t, GRAMS * (t + 1)):
                    act.wait_ge(gram_done, gi + 1)
                    move_products(act, copy, gi, (2, 3), main_act, z_act)
                ahead = iter(range(NG) if t + 1 < TILES else ())

                def move_ahead(count):
                    for _, g in zip(range(count), ahead):
                        move_group(t + 1, g)

                move_ahead(1)
                act.wait_ge(vec_ready, 1)
                act.wait_ge(l1_done, 2 * t + 1)
                for o in range(HALF1):
                    last = act.activation(h1[:, t % 2, o, :], l1_ps(o), ACT.Relu, bias=vec[:, o:o + 1])
                last.then_inc(h1_act, 1)
                move_ahead(1)
                act.wait_ge(l2_done, 2 * t + 1)
                for o in range(HALF2):
                    last = act.activation(h2[:, t % 2, o, :], l2_ps(o), ACT.Relu,
                                          bias=vec[:, OC1 + o:OC1 + o + 1])
                last.then_inc(h2_act, 1)
                move_ahead(1)
                act.wait_ge(l3_done, t + 1)
                copy(y_sb[:, t * P:(t + 1) * P], l3_ps).then_inc(y_ready, 1)
                move_ahead(NG)

        @block.vector
        def _(dve):
            def copy(out, in_):
                return dve.tensor_copy(out, in_)

            def low_part(n):
                dve.wait_ge(hi_ready, n + 1)
                if n >= 2:
                    dve.wait_ge(one_hot_used, CHUNKS_BEFORE[n - 1])
                dve.tensor_tensor(table_lo[0:TP, n % 2, 0:TC[n], :], table_sb[0:TP, n % 3, 0:TC[n], :],
                                  table_hi[0:TP, n % 2, 0:TC[n], :], ALU.subtract).then_inc(lo_ready, 1)

            def one_hots(n):
                dve.wait_ge(offset_ready, n + 1)
                for c in range(TC[n]):
                    m = CHUNKS_BEFORE[n] + c
                    if m >= OH_RING:
                        dve.wait_ge(one_hot_used, m - OH_RING + 1)
                    dve.tensor_scalar(one_hot[0:TP, m % OH_RING, :], offset16[0:TP, n % 2, :], float(c), None,
                                      ALU.is_equal).then_inc(one_hot_ready, 1)

            def move_group(t, g):
                n = tr_number(t, g)
                if n % 2 == 1:
                    dve.wait_ge(tr_done, n + 1)
                    move_transposed(copy, t, g).then_inc(tr_moved_dve, 1)

            dve.memset(w1_pairs[:], 0.0).then_inc(w1_zeroed, 1)
            dve.memset(et[:, :, DUP + F:ROWS], 0.0).then_inc(et_padded, 1)
            dve.wait_ge(ident_ready, 1)
            copy(ident16[:], ident[:]).then_inc(ident16_ready, 1)
            dve.wait_ge(ids_loaded, 16)
            copy(ids16[:], ids_sb[:, :, ONE_HOT[0]:ONE_HOT[-1] + 1]).then_inc(ids16_ready, 1)
            for n in range(NOH):
                low_part(n)
                one_hots(n)
            dve.wait_ge(wd_loaded, 32)
            dve.tensor_tensor(w1_dense_sum[:], w1_dense[:, 0, :], w1_dense[:, 1, :], ALU.add).then_inc(wd_ready, 1)

            for g in range(NG):
                move_group(0, g)
            for t in range(TILES):
                for gi in range(GRAMS * t, GRAMS * (t + 1)):
                    dve.wait_ge(gram_done, gi + 1)
                    move_products(dve, copy, gi, (0, 1), main_dve, z_dve)
                ahead = iter(range(NG) if t + 1 < TILES else ())

                def move_ahead(count):
                    for _, g in zip(range(count), ahead):
                        move_group(t + 1, g)

                move_ahead(1)
                dve.wait_ge(vec_ready, 1)
                dve.wait_ge(l1_done, 2 * t + 2)
                for o in range(HALF1, OC1):
                    last = dve.tensor_scalar(h1[:, t % 2, o, :], l1_ps(o), vec[:, o:o + 1], 0.0,
                                             ALU.add, ALU.max)
                last.then_inc(h1_dve, 1)
                move_ahead(1)
                dve.wait_ge(l2_done, 2 * t + 2)
                for o in range(HALF2, OC2):
                    last = dve.tensor_scalar(h2[:, t % 2, o, :], l2_ps(o), vec[:, OC1 + o:OC1 + o + 1], 0.0,
                                             ALU.add, ALU.max)
                last.then_inc(h2_dve, 1)
                move_ahead(NG)

        @block.tensor
        def _(pe):
            def spread(n):
                if n >= 2:
                    pe.wait_ge(offset_ready, n - 1)
                for t in range(TILES):
                    last = pe.matmul(spread_bank(n)[:, t * P:(t + 1) * P],
                                     ids16[:, t, n:n + 1].to_broadcast([P, P]), ident16[:],
                                     start=True, stop=True)
                last.then_inc(spread_done, 1)

            def look_up(n):
                pe.wait_ge(lo_ready, n + 1)
                if n >= 2:
                    pe.wait_ge(sum_moved, n - 1)
                for c in range(TC[n]):
                    m = CHUNKS_BEFORE[n] + c
                    pe.wait_ge(one_hot_ready, m + 1)
                    pe.matmul(sum_bank(n), table_hi[0:TP, n % 2, c, :], one_hot[0:TP, m % OH_RING, :],
                              start=c == 0, stop=False)
                    last = pe.matmul(sum_bank(n), table_lo[0:TP, n % 2, c, :], one_hot[0:TP, m % OH_RING, :],
                                     start=False, stop=c == TC[n] - 1)
                    last.then_inc(one_hot_used, 1)

            def transposes(t, g):
                n = tr_number(t, g)
                pe.wait_ge(gathered[t][g], 16 * len(GROUPS[g]))
                if n >= 2:
                    if n % 2:
                        pe.wait_ge(tr_moved_dve, moved_by_dve(n - 2))
                    else:
                        pe.wait_ge(tr_moved_act, moved_by_act(n - 2))
                for place, k in enumerate(GROUPS[g]):
                    last = pe.transpose(tr_bank(n)[:, place * P:(place + 1) * P],
                                        rows[:, t % 2, GATHERED.index(k), :], ident[:])
                last.then_inc(tr_done, 1)

            def gram(t):
                if t == 0:
                    pe.wait_ge(et_padded, 1)
                pe.wait_ge(tr_moved_act, moved_by_act(tr_number(t, NG - 1)))
                pe.wait_ge(tr_moved_dve, moved_by_dve(tr_number(t, NG - 1)))
                for gi in range(GRAMS * t, GRAMS * (t + 1)):
                    if gi >= 2:
                        pe.wait_ge(z_act, gi - 1)
                        pe.wait_ge(z_dve, gi - 1)
                    for m in range(GROUP_BLOCKS):
                        b0 = gi * GROUP_ROWS + m * BLOCK
                        bank, at = divmod(m, BLOCKS_PER_BANK)
                        out = ps[:, GRAM_BANKS * (gi % 2) + bank, at * BLOCK * MOV:(at + 1) * BLOCK * MOV]
                        last = pe.matmul(out, et[:, b0:b0 + BLOCK, 0:ROWS], et[:, b0:b0 + BLOCK, DUP + 1:DUP + F],
                                         start=True, stop=True)
                    last.then_inc(gram_done, 1)

            def layer1(t):
                if t == 0:
                    pe.wait_ge(vec_ready, 1)
                    pe.wait_ge(wd_ready, 1)
                    pe.wait_ge(w1_loaded, 16 * len(PIECES))
                pe.wait_ge(z_act, GRAMS * (t + 1))
                pe.wait_ge(z_dve, GRAMS * (t + 1))
                if t >= 1:
                    pe.wait_ge(y_ready, t)
                    pe.wait_ge(h2_dve, t)
                for o in range(OC1):
                    cols = slice(o * P, (o + 1) * P)
                    pe.matmul(l1_ps(o), w1_dense_sum[:, cols], xt[:, t * P:(t + 1) * P],
                              start=True, stop=False)
                    for c in range(CHUNKS):
                        last = pe.matmul(l1_ps(o), w1_pairs[:, c, cols], z[:, c, t * P:(t + 1) * P],
                                         start=False, stop=c == CHUNKS - 1)
                    if o % HALF1 == HALF1 - 1:
                        last.then_inc(l1_done, 1)

            def layer2(t):
                if t == 0:
                    pe.wait_ge(w2_loaded, 16)
                pe.wait_ge(h1_act, t + 1)
                pe.wait_ge(h1_dve, t + 1)
                for o in range(OC2):
                    for k in range(OC1):
                        last = pe.matmul(l2_ps(o), w2_sb[:, k, o * P:(o + 1) * P], h1[:, t % 2, k, :],
                                         start=k == 0, stop=k == OC1 - 1)
                    if o % HALF2 == HALF2 - 1:
                        last.then_inc(l2_done, 1)

            def layer3(t):
                pe.wait_ge(h2_act, t + 1)
                pe.wait_ge(h2_dve, t + 1)
                for k in range(OC2):
                    last = pe.matmul(l3_ps, vec[:, OC1 + OC2 + k:OC1 + OC2 + k + 1], h2[:, t % 2, k, :],
                                     start=k == 0, stop=k == OC2 - 1)
                last.then_inc(l3_done, 1)

            pe.wait_ge(ident16_ready, 1)
            pe.wait_ge(ids16_ready, 1)
            spread(0)
            spread(1)
            pe.wait_ge(ident_ready, 1)
            pe.wait_ge(x_loaded, 16)
            for t in range(TILES):
                last = pe.transpose(tr_bank(0)[:, t * P:(t + 1) * P], x_sb[:, t, :], ident[:])
            last.then_inc(tr_done, 1)
            pe.wait_ge(vec_loaded, 48)
            pe.transpose(vec_ps, vec_rows[:], ident[0:NVEC, 0:NVEC]).then_inc(vec_done, 1)
            for n in range(NOH):
                look_up(n)
                if n + 2 < NOH:
                    spread(n + 2)
            pe.wait_ge(sum_moved, NOH)
            for g in range(NG):
                transposes(0, g)
            for t in range(TILES):
                gram(t)
                ahead = iter(range(NG) if t + 1 < TILES else ())
                for step, count in ((layer1, 1), (layer2, 1), (layer3, 1), (None, NG)):
                    for _, g in zip(range(count), ahead):
                        transposes(t + 1, g)
                    if step:
                        step(t)


_TABLES = [f"tbl_{k}" for k in range(26)]
_INS = ["r_dense_features", "ids", *_TABLES, "W_top1", "b_top1", "W_top2", "b_top2", "W_top3"]


def kernel(**inputs):
    import numpy as _np
    import concourse.bacc as _bacc
    from concourse.bass_utils import run_bass_kernel_spmd as _run

    nc = _bacc.Bacc("TRN2", target_bir_lowering=False, num_devices=1)
    arrays, aps = {}, {}
    for name in _INS:
        a = _np.ascontiguousarray(inputs[name])
        arrays[f"in_{name}"] = a
        aps[name] = nc.dram_tensor(f"in_{name}", a.shape, mybir.dt.from_np(a.dtype), kind="ExternalInput").ap()
    batch = aps["ids"].shape[0]
    y = nc.dram_tensor("out_y", (batch, 1), F32, kind="ExternalOutput").ap()
    dlrm_program(nc, aps["r_dense_features"], aps["ids"], [aps[n] for n in _TABLES], aps["W_top1"],
                 aps["b_top1"], aps["W_top2"], aps["b_top2"], aps["W_top3"], y)
    r = _run(nc, [arrays], core_ids=[0])
    return r.results[0]["out_y"]
```

```python
import concourse.bass as bass
from concourse import mybir
from concourse.alu_op_type import AluOpType as ALU
from contextlib import ExitStack

F32 = mybir.dt.float32
F32R = mybir.dt.float32r
F16 = mybir.dt.float16
I32 = mybir.dt.int32
ACT = mybir.ActivationFunctionType

P = 128


def dlrm_program(nc, dense, ids, tables, w1, b1, w2, b2, w3, y_out):
    B, D = dense.shape
    NTAB = len(tables)
    F = NTAB + 1
    O1, O2 = w2.shape
    PAIRS = F * (F - 1) // 2
    TILES = B // P
    OC1, OC2 = O1 // P, O2 // P
    assert D == P and F == 27 and w1.shape[0] == D + PAIRS + D

    ROWS = 32
    QUADS = P // ROWS
    MOV = F - 1
    CHUNKS = MOV // QUADS
    DUP = MOV - CHUNKS * QUADS
    FIRST_MAIN = DUP + 1
    assert DUP + F <= ROWS

    FIRST_SMALL = 19
    ONE_HOT = sorted(range(FIRST_SMALL, NTAB), key=lambda k: tables[k].shape[0])
    GATHERED = [k for k in range(NTAB) if k not in ONE_HOT]
    NOH = len(ONE_HOT)
    TP = 125
    TC = [tables[k].shape[0] // TP for k in ONE_HOT]
    TC_MAX = max(TC)
    assert all(tables[k].shape[0] == TP * c for k, c in zip(ONE_HOT, TC))
    assert all(tables[k].shape[0] <= 2048 for k in ONE_HOT)
    OH_RING = 8
    HALVES = 2
    CHUNKS_BEFORE = [sum(TC[:n]) for n in range(NOH + 1)]

    GROUPS = [GATHERED[n:n + 4] for n in range(0, len(GATHERED), 4)]
    NG = len(GROUPS)
    FIRST_BETWEEN = NOH - NG
    assert FIRST_BETWEEN >= 0

    BLOCK = 4
    BLOCKS_PER_BANK = 4
    GRAM_BANKS = 2
    GROUP_BLOCKS = BLOCKS_PER_BANK * GRAM_BANKS
    GROUP_ROWS = GROUP_BLOCKS * BLOCK
    GRAMS = P // GROUP_ROWS

    def pair_row(i, j):
        return D + i * F - i * (i + 1) // 2 + (j - i - 1)

    ctx = ExitStack()
    with ctx:
        def sb(name, shape, dt):
            return ctx.enter_context(nc.sbuf_tensor(name, shape, dt))

        def sem(name):
            return ctx.enter_context(nc.semaphore(name))

        et = sb("et", [P, B, ROWS], F32)
        xt = sb("xt", [P, B], F32)
        z = sb("z", [P, CHUNKS, B], F32)
        rows = sb("rows", [P, 2, len(GATHERED), D], F32)
        x_sb = sb("x_sb", [P, TILES, D], F32)
        ids_sb = sb("ids_sb", [P, TILES, NTAB], I32)
        ids16 = sb("ids16", [P, TILES, NOH], F16)
        ident = sb("ident", [P, P], F32)
        ident16 = sb("ident16", [P, P], F16)
        first_row = sb("first_row", [P, 3], F32)
        table_sb = sb("table_sb", [P, 3, TC_MAX, D], F32)
        table_hi = sb("table_hi", [P, 3, TC_MAX, D], F32R)
        table_lo = sb("table_lo", [P, 3, TC_MAX, D], F32R)
        offset16 = sb("offset16", [P, 2, B], F16)
        one_hot = sb("one_hot", [P, OH_RING, B], F32R)
        w1_pairs = sb("w1_pairs", [P, CHUNKS, O1], F32)
        w1_dense = sb("w1_dense", [P, 2, O1], F32)
        w1_dense_sum = sb("w1_dense_sum", [P, O1], F32)
        w2_sb = sb("w2_sb", [P, OC1, O2], F32)
        NVEC = OC1 + 2 * OC2
        vec_rows = sb("vec_rows", [NVEC, P], F32)
        vec = sb("vec", [P, NVEC], F32)
        h1 = sb("h1", [P, 2, OC1, P], F32)
        h2 = sb("h2", [P, 2, OC2, P], F32)
        y_sb = sb("y_sb", [1, B], F32)
        ps = ctx.enter_context(nc.psum_tensor("ps", [P, 8, 512], F32))

        def sum_bank(n):
            return ps[:, 2 * (n % 2), :]

        def spread_bank(n):
            return ps[:, 2 * (n % 2) + 1, :]

        def tr_bank(n):
            return ps[:, 4 + n % 2, :]

        HALF1, HALF2 = OC1 // 2, OC2 // 2

        def l1_ps(o):
            return ps[:, 6 + o // HALF1, o % HALF1 * P:(o % HALF1 + 1) * P]

        def l2_ps(o):
            at = HALF1 + o % HALF2
            return ps[:, 6 + o // HALF2, at * P:(at + 1) * P]

        l3_ps = ps[0:1, 6, (HALF1 + HALF2) * P:(HALF1 + HALF2 + 1) * P]
        vec_ps = ps[:, 7, 0:NVEC]

        ids_loaded, x_loaded, vec_loaded = sem("ids_loaded"), sem("x_loaded"), sem("vec_loaded")
        wd_loaded, w2_loaded, w1_loaded = sem("wd_loaded"), sem("w2_loaded"), sem("w1_loaded")
        table_loaded = [[sem(f"table_loaded{n}_{h}") for h in range(HALVES)] for n in range(NOH)]
        gathered = [[sem(f"gathered{t}_{g}") for g in range(NG)] for t in range(TILES)]
        y_stored = sem("y_stored")
        ident_zero, ident_ready, first_row_ready = sem("ident_zero"), sem("ident_ready"), sem("first_row_ready")
        w1_zeroed, wd_ready, et_padded = sem("w1_zeroed"), sem("wd_ready"), sem("et_padded")
        ids16_ready, ident16_ready = sem("ids16_ready"), sem("ident16_ready")
        spread_done, offset_ready = sem("spread_done"), sem("offset_ready")
        hi_ready, lo_ready = sem("hi_ready"), sem("lo_ready")
        one_hot_ready, one_hot_used = sem("one_hot_ready"), sem("one_hot_used")
        sum_moved = sem("sum_moved")
        tr_done, tr_moved_act, tr_moved_dve = sem("tr_done"), sem("tr_moved_act"), sem("tr_moved_dve")
        vec_done, vec_ready = sem("vec_done"), sem("vec_ready")
        gram_done = sem("gram_done")
        main_act, main_dve, z_act, z_dve = sem("main_act"), sem("main_dve"), sem("z_act"), sem("z_dve")
        l1_done, h1_act, h1_dve = sem("l1_done"), sem("h1_act"), sem("h1_dve")
        l2_done, h2_act, h2_dve = sem("l2_done"), sem("h2_act"), sem("h2_dve")
        l3_done, y_ready = sem("l3_done"), sem("y_ready")

        def tr_number(t, g):
            return 1 + t * NG + g

        def moved_by_act(n):
            return n // 2 + 1

        def moved_by_dve(n):
            return (n + 1) // 2

        def between(t, o):
            if t + 1 == TILES:
                return ()
            return (0, 1) if o == 0 else range(o + 1, NG if o == OC1 - 1 else o + 2)

        def half(n, h):
            return slice(h * TC[n] // HALVES, (h + 1) * TC[n] // HALVES)

        def w1_pieces():
            for i in range(F - 1):
                skip = max(0, i + 1 - FIRST_MAIN)
                g, c = divmod(skip, CHUNKS)
                if c:
                    yield g, 1, DUP + i, c, CHUNKS - c, pair_row(i, FIRST_MAIN + skip)
                    g += 1
                if g < QUADS:
                    yield g, QUADS - g, DUP + i, 0, CHUNKS, pair_row(i, FIRST_MAIN + CHUNKS * g)
            for i in range(DUP):
                yield 0, 1, i, i, DUP - i, pair_row(i, i + 1)

        PIECES = list(w1_pieces())
        SHARE = 4

        block = ctx.enter_context(nc.Block())

        @block.sync
        def _(sp):
            def load_table(n):
                if n >= 3:
                    sp.wait_ge(lo_ready, HALVES * (n - 2))
                src = tables[ONE_HOT[n]].rearrange("(p c) d -> p c d", p=TP)
                for h in range(HALVES):
                    sp.dma_start(table_sb[0:TP, n % 3, half(n, h), :], src[:, half(n, h), :])\
                      .then_inc(table_loaded[n][h], 16)

            def load_w1(pieces):
                for g, ng, p, c, nc_, row in pieces:
                    src = w1[row:row + ng * nc_, :].rearrange("(g c) o -> g c o", g=ng)
                    first = ROWS * g + p
                    dst = w1_pairs[first:first + ROWS * (ng - 1) + 1:ROWS, c:c + nc_, :]
                    sp.dma_start(dst, src).then_inc(w1_loaded, 16)

            sp.dma_start(ids_sb[:], ids.rearrange("(t p) k -> p t k", p=P)).then_inc(ids_loaded, 16)
            load_table(0)
            load_table(1)
            sp.dma_start(x_sb[:], dense.rearrange("(t p) d -> p t d", p=P)).then_inc(x_loaded, 16)
            load_table(2)
            sp.dma_start(vec_rows[0:OC1, :], b1.rearrange("(o p) -> o p", p=P)).then_inc(vec_loaded, 16)
            sp.dma_start(vec_rows[OC1:OC1 + OC2, :], b2.rearrange("(o p) -> o p", p=P)).then_inc(vec_loaded, 16)
            sp.dma_start(vec_rows[OC1 + OC2:NVEC, :],
                         w3.rearrange("(o p) u -> o (p u)", p=P)).then_inc(vec_loaded, 16)
            sp.wait_ge(w1_zeroed, 1)
            for n in range(3, NOH):
                load_table(n)
                load_w1(PIECES[(n - 3) * SHARE:(n - 2) * SHARE])
            load_w1(PIECES[(NOH - 3) * SHARE:])
            sp.dma_start(w1_dense[:, 0, :], w1[0:D, :]).then_inc(wd_loaded, 16)
            sp.dma_start(w1_dense[:, 1, :], w1[D + PAIRS:D + PAIRS + D, :]).then_inc(wd_loaded, 16)
            sp.dma_start(w2_sb[:], w2.rearrange("(k p) o -> p k o", p=P)).then_inc(w2_loaded, 16)
            sp.wait_ge(y_ready, TILES)
            sp.dma_start(y_out.rearrange("b u -> u b"), y_sb[:]).then_inc(y_stored, 16)
            sp.wait_ge(y_stored, 16)

        @block.gpsimd
        def _(pool):
            pool.memset(ident[:], 0.0).then_inc(ident_zero, 1)
            pool.wait_ge(ident_zero, 1)
            pool.affine_select(out=ident[:], in_=ident[:], compare_op=ALU.not_equal, fill=1.0, base=0,
                               pattern=[[-1, P]], channel_multiplier=1).then_inc(ident_ready, 1)
            for n, c in enumerate(sorted(set(TC))):
                pool.iota(first_row[:, n:n + 1], pattern=[[0, 1]], base=0, channel_multiplier=-c,
                          allow_small_or_imprecise_dtypes=True).then_inc(first_row_ready, 1)
            pool.wait_ge(ids_loaded, 16)
            for t in range(TILES):
                for g, group in enumerate(GROUPS):
                    if t >= 2:
                        pool.wait_ge(tr_done, tr_number(t - 2, g) + 1)
                    for k in group:
                        pool.indirect_dma_start(
                            rows[:, t % 2, GATHERED.index(k), :], None, tables[k],
                            bass.IndirectOffsetOnAxis(ids_sb[:, t, k:k + 1], 0),
                        ).then_inc(gathered[t][g], 16)

        def runs(t, g):
            features = [k + 1 for k in GROUPS[g]]
            start = 0
            for n in range(1, len(features) + 1):
                if n == len(features) or features[n] != features[n - 1] + 1:
                    yield features[start], features[n - 1] + 1, start, DUP + features[start]
                    start = n
            again = [f for f in features if f < DUP]
            if again:
                yield again[0], again[-1] + 1, features.index(again[0]), again[0]

        def move_transposed(copy, t, g):
            bank = tr_bank(tr_number(t, g))
            for f, f_end, place, col in runs(t, g):
                n = f_end - f
                last = copy(et[:, t * P:(t + 1) * P, col:col + n].rearrange("p b f -> p f b"),
                            bank[:, place * P:(place + n) * P].rearrange("p (f b) -> p f b", f=n))
            return last

        def products(gi, q, w, n):
            b = GRAM_BANKS * (gi % 2)
            width = BLOCK * MOV
            v = ps[ROWS * q:ROWS * (q + 1), b:b + GRAM_BANKS, 0:BLOCKS_PER_BANK * width]
            v = v.rearrange("p k (m w) -> p k m w", m=BLOCKS_PER_BANK)
            return v[:, :, :, MOV * q + w:MOV * q + w + n]

        def slots(gi, q, g, c, n):
            b0 = gi * GROUP_ROWS
            v = z[ROWS * g:ROWS * (g + 1), c:c + n, b0:b0 + GROUP_ROWS]
            v = v.rearrange("p c (k m q) -> p k m c q", k=GRAM_BANKS, m=BLOCKS_PER_BANK)
            return v[:, :, :, :, q]

        def move_products(eng, copy, gi, quads, main_sem, z_sem):
            for g in range(QUADS):
                for q in quads:
                    copy(slots(gi, q, g, 0, CHUNKS),
                         products(gi, q, FIRST_MAIN - 1 + CHUNKS * g, CHUNKS)).then_inc(main_sem, 1)
            eng.wait_ge(main_sem, len(quads) * (QUADS * gi + 1))
            for q in quads:
                last = copy(slots(gi, q, 0, 0, DUP)[0:DUP], products(gi, q, 0, DUP)[0:DUP])
            last.then_inc(z_sem, 1)

        @block.scalar
        def _(act):
            def copy(out, in_):
                return act.activation(out, in_, ACT.Copy)

            def high_part(n):
                if n >= 3:
                    act.wait_ge(one_hot_used, CHUNKS_BEFORE[n - 2])
                for h in range(HALVES):
                    act.wait_ge(table_loaded[n][h], 16)
                    copy(table_hi[0:TP, n % 3, half(n, h), :],
                         table_sb[0:TP, n % 3, half(n, h), :]).then_inc(hi_ready, 1)

            def offsets(n):
                act.wait_ge(spread_done, n + 1)
                if n >= 2:
                    act.wait_ge(one_hot_ready, CHUNKS_BEFORE[n - 1])
                which = sorted(set(TC)).index(TC[n])
                act.activation(offset16[0:TP, n % 2, :], spread_bank(n)[0:TP, :], ACT.Identity,
                               bias=first_row[0:TP, which:which + 1]).then_inc(offset_ready, 1)

            def move_sum(n):
                act.wait_ge(one_hot_used, CHUNKS_BEFORE[n + 1])
                col = DUP + ONE_HOT[n] + 1
                copy(et[:, :, col], sum_bank(n)).then_inc(sum_moved, 1)

            def move_group(t, g):
                n = tr_number(t, g)
                if n % 2 == 0:
                    act.wait_ge(tr_done, n + 1)
                    move_transposed(copy, t, g).then_inc(tr_moved_act, 1)

            def relu1(t):
                act.wait_ge(l1_done, 2 * t + 1)
                for o in range(HALF1):
                    last = act.activation(h1[:, t % 2, o, :], l1_ps(o), ACT.Relu, bias=vec[:, o:o + 1])
                last.then_inc(h1_act, 1)

            def relu2(t):
                act.wait_ge(l2_done, 2 * t + 1)
                for o in range(HALF2):
                    last = act.activation(h2[:, t % 2, o, :], l2_ps(o), ACT.Relu,
                                          bias=vec[:, OC1 + o:OC1 + o + 1])
                last.then_inc(h2_act, 1)

            def move_y(t):
                act.wait_ge(l3_done, t + 1)
                copy(y_sb[:, t * P:(t + 1) * P], l3_ps).then_inc(y_ready, 1)

            act.wait_ge(first_row_ready, len(set(TC)))
            copy(first_row[:, 2:3], first_row[:, 0:1])
            high_part(0)
            offsets(0)
            high_part(1)
            offsets(1)
            high_part(2)
            act.wait_ge(ident_ready, 1)
            act.activation(w1_pairs[:].rearrange("p c (n o) -> p (c n) o", o=P),
                           ident[:, None, :].to_broadcast([P, CHUNKS * OC1, P]), ACT.Copy,
                           scale=0.0).then_inc(w1_zeroed, 1)
            act.wait_ge(tr_done, 1)
            copy(xt[:], tr_bank(0))
            copy(et[:, :, 0], tr_bank(0))
            copy(et[:, :, DUP], tr_bank(0)).then_inc(tr_moved_act, 1)
            act.wait_ge(vec_done, 1)
            copy(vec[:], vec_ps).then_inc(vec_ready, 1)
            for n in range(NOH):
                move_sum(n)
                if n >= FIRST_BETWEEN:
                    move_group(0, n - FIRST_BETWEEN)
                if n + 2 < NOH:
                    offsets(n + 2)
                if n + 3 < NOH:
                    high_part(n + 3)
                if n == 0:
                    act.wait_ge(tr_moved_act, 1)
                    copy(et[:, :, DUP + F:ROWS].rearrange("p b f -> p f b"),
                         xt[:, None, :].to_broadcast([P, ROWS - DUP - F, B])).then_inc(et_padded, 1)

            act.wait_ge(vec_ready, 1)
            for t in range(TILES):
                for m in range(GRAMS):
                    gi = GRAMS * t + m
                    act.wait_ge(gram_done, gi + 1)
                    move_products(act, copy, gi, (2, 3), main_act, z_act)
                    if t >= 1 and m == 0:
                        relu2(t - 1)
                    if t >= 1 and m == 1:
                        move_y(t - 1)
                for o in range(OC1):
                    for g in between(t, o):
                        move_group(t + 1, g)
                    if o == HALF1 - 1:
                        relu1(t)
            relu2(TILES - 1)
            move_y(TILES - 1)

        @block.vector
        def _(dve):
            def copy(out, in_):
                return dve.tensor_copy(out, in_)

            def low_part(n):
                if n >= 3:
                    dve.wait_ge(one_hot_used, CHUNKS_BEFORE[n - 2])
                for h in range(HALVES):
                    dve.wait_ge(hi_ready, HALVES * n + h + 1)
                    dve.tensor_tensor(table_lo[0:TP, n % 3, half(n, h), :], table_sb[0:TP, n % 3, half(n, h), :],
                                      table_hi[0:TP, n % 3, half(n, h), :], ALU.subtract).then_inc(lo_ready, 1)

            def one_hots(n):
                dve.wait_ge(offset_ready, n + 1)
                for c in range(TC[n]):
                    m = CHUNKS_BEFORE[n] + c
                    if m >= OH_RING:
                        dve.wait_ge(one_hot_used, m - OH_RING + 1)
                    dve.tensor_scalar(one_hot[0:TP, m % OH_RING, :], offset16[0:TP, n % 2, :], float(c), None,
                                      ALU.is_equal).then_inc(one_hot_ready, 1)

            def move_group(t, g):
                n = tr_number(t, g)
                if n % 2 == 1:
                    dve.wait_ge(tr_done, n + 1)
                    move_transposed(copy, t, g).then_inc(tr_moved_dve, 1)

            def relu1(t):
                dve.wait_ge(l1_done, 2 * t + 2)
                for o in range(HALF1, OC1):
                    last = dve.tensor_scalar(h1[:, t % 2, o, :], l1_ps(o), vec[:, o:o + 1], 0.0,
                                             ALU.add, ALU.max)
                last.then_inc(h1_dve, 1)

            def relu2(t):
                dve.wait_ge(l2_done, 2 * t + 2)
                for o in range(HALF2, OC2):
                    last = dve.tensor_scalar(h2[:, t % 2, o, :], l2_ps(o), vec[:, OC1 + o:OC1 + o + 1], 0.0,
                                             ALU.add, ALU.max)
                last.then_inc(h2_dve, 1)

            dve.wait_ge(ident_ready, 1)
            copy(ident16[:], ident[:]).then_inc(ident16_ready, 1)
            dve.wait_ge(ids_loaded, 16)
            copy(ids16[:], ids_sb[:, :, FIRST_SMALL:]).then_inc(ids16_ready, 1)
            for n in range(NOH):
                low_part(n)
                one_hots(n)
                if n - 1 >= FIRST_BETWEEN:
                    move_group(0, n - 1 - FIRST_BETWEEN)
            move_group(0, NG - 1)

            dve.wait_ge(vec_ready, 1)
            for t in range(TILES):
                for m in range(GRAMS):
                    gi = GRAMS * t + m
                    dve.wait_ge(gram_done, gi + 1)
                    move_products(dve, copy, gi, (0, 1), main_dve, z_dve)
                    if t >= 1 and m == 0:
                        relu2(t - 1)
                if t == 0:
                    dve.wait_ge(wd_loaded, 32)
                    dve.tensor_tensor(w1_dense_sum[:], w1_dense[:, 0, :], w1_dense[:, 1, :],
                                      ALU.add).then_inc(wd_ready, 1)
                for o in range(OC1):
                    for g in between(t, o):
                        move_group(t + 1, g)
                relu1(t)
            relu2(TILES - 1)

        @block.tensor
        def _(pe):
            def spread(n):
                if n >= 2:
                    pe.wait_ge(offset_ready, n - 1)
                for t in range(TILES):
                    last = pe.matmul(spread_bank(n)[:, t * P:(t + 1) * P],
                                     ids16[:, t, ONE_HOT[n] - FIRST_SMALL:ONE_HOT[n] - FIRST_SMALL + 1].to_broadcast([P, P]), ident16[:],
                                     start=True, stop=True)
                last.then_inc(spread_done, 1)

            def look_up(n):
                if n >= 2:
                    pe.wait_ge(sum_moved, n - 1)
                for c in range(TC[n]):
                    m = CHUNKS_BEFORE[n] + c
                    for h in range(HALVES):
                        if c == half(n, h).start:
                            pe.wait_ge(lo_ready, HALVES * n + h + 1)
                    pe.wait_ge(one_hot_ready, m + 1)
                    pe.matmul(sum_bank(n), table_hi[0:TP, n % 3, c, :], one_hot[0:TP, m % OH_RING, :],
                              start=c == 0, stop=False)
                    last = pe.matmul(sum_bank(n), table_lo[0:TP, n % 3, c, :], one_hot[0:TP, m % OH_RING, :],
                                     start=False, stop=c == TC[n] - 1)
                    last.then_inc(one_hot_used, 1)

            def transposes(t, g):
                n = tr_number(t, g)
                pe.wait_ge(gathered[t][g], 16 * len(GROUPS[g]))
                if n >= 2:
                    if n % 2:
                        pe.wait_ge(tr_moved_dve, moved_by_dve(n - 2))
                    else:
                        pe.wait_ge(tr_moved_act, moved_by_act(n - 2))
                for place, k in enumerate(GROUPS[g]):
                    last = pe.transpose(tr_bank(n)[:, place * P:(place + 1) * P],
                                        rows[:, t % 2, GATHERED.index(k), :], ident[:])
                last.then_inc(tr_done, 1)

            def features_ready(t):
                if t == 0:
                    pe.wait_ge(et_padded, 1)
                    pe.wait_ge(sum_moved, NOH)
                pe.wait_ge(tr_moved_act, moved_by_act(tr_number(t, NG - 1)))
                pe.wait_ge(tr_moved_dve, moved_by_dve(tr_number(t, NG - 1)))

            def gram(gi):
                if gi >= 2:
                    pe.wait_ge(z_act, gi - 1)
                    pe.wait_ge(z_dve, gi - 1)
                for m in range(GROUP_BLOCKS):
                    b0 = gi * GROUP_ROWS + m * BLOCK
                    bank, at = divmod(m, BLOCKS_PER_BANK)
                    out = ps[:, GRAM_BANKS * (gi % 2) + bank, at * BLOCK * MOV:(at + 1) * BLOCK * MOV]
                    last = pe.matmul(out, et[:, b0:b0 + BLOCK, 0:ROWS], et[:, b0:b0 + BLOCK, DUP + 1:DUP + F],
                                     start=True, stop=True)
                last.then_inc(gram_done, 1)

            def layer1_dense(t, o):
                pe.matmul(l1_ps(o), w1_dense_sum[:, o * P:(o + 1) * P], xt[:, t * P:(t + 1) * P],
                          start=True, stop=False)

            def layer1_ready(t):
                if t == 0:
                    pe.wait_ge(vec_ready, 1)
                    pe.wait_ge(wd_ready, 1)
                    pe.wait_ge(w1_loaded, 16 * len(PIECES))
                if t >= 1:
                    pe.wait_ge(y_ready, t)
                    pe.wait_ge(h2_dve, t)
                layer1_dense(t, 0)
                layer1_dense(t, HALF1)
                pe.wait_ge(z_act, GRAMS * (t + 1))
                pe.wait_ge(z_dve, GRAMS * (t + 1))

            def layer1(t, o):
                if o % HALF1:
                    layer1_dense(t, o)
                for c in range(CHUNKS):
                    last = pe.matmul(l1_ps(o), w1_pairs[:, c, o * P:(o + 1) * P], z[:, c, t * P:(t + 1) * P],
                                     start=False, stop=c == CHUNKS - 1)
                if o % HALF1 == HALF1 - 1:
                    last.then_inc(l1_done, 1)

            def layer2(t):
                if t == 0:
                    pe.wait_ge(w2_loaded, 16)
                pe.wait_ge(h1_act, t + 1)
                for o in range(OC2):
                    for k in range(OC1):
                        if o == 0 and k == HALF1:
                            pe.wait_ge(h1_dve, t + 1)
                        last = pe.matmul(l2_ps(o), w2_sb[:, k, o * P:(o + 1) * P], h1[:, t % 2, k, :],
                                         start=k == 0, stop=k == OC1 - 1)
                    if o % HALF2 == HALF2 - 1:
                        last.then_inc(l2_done, 1)

            def layer3(t):
                pe.wait_ge(h2_act, t + 1)
                for k in range(OC2):
                    if k == HALF2:
                        pe.wait_ge(h2_dve, t + 1)
                    last = pe.matmul(l3_ps, vec[:, OC1 + OC2 + k:OC1 + OC2 + k + 1], h2[:, t % 2, k, :],
                                     start=k == 0, stop=k == OC2 - 1)
                last.then_inc(l3_done, 1)

            def small_transposes():
                pe.wait_ge(ident_ready, 1)
                pe.wait_ge(x_loaded, 16)
                for t in range(TILES):
                    last = pe.transpose(tr_bank(0)[:, t * P:(t + 1) * P], x_sb[:, t, :], ident[:])
                last.then_inc(tr_done, 1)
                pe.wait_ge(vec_loaded, 48)
                pe.transpose(vec_ps, vec_rows[:], ident[0:NVEC, 0:NVEC]).then_inc(vec_done, 1)

            def warm_up(n):
                for _ in range(n):
                    pe.matmul(ps[:, 6, 0:P], ident16[:], ident16[:], start=True, stop=True)

            pe.wait_ge(ident16_ready, 1)
            warm_up(14)
            pe.wait_ge(ids16_ready, 1)
            spread(0)
            spread(1)
            warm_up(16)
            for n in range(NOH):
                look_up(n)
                if n == 0:
                    small_transposes()
                if n + 2 < NOH:
                    spread(n + 2)
                if n >= FIRST_BETWEEN:
                    transposes(0, n - FIRST_BETWEEN)
            for t in range(TILES):
                features_ready(t)
                for m in range(GRAMS):
                    gram(GRAMS * t + m)
                    if t >= 1 and m == 0:
                        layer2(t - 1)
                    if t >= 1 and m == 1:
                        layer3(t - 1)
                for o in range(OC1):
                    for g in between(t, o):
                        transposes(t + 1, g)
                    if o == 0:
                        layer1_ready(t)
                    layer1(t, o)
            layer2(TILES - 1)
            layer3(TILES - 1)


_TABLES = [f"tbl_{k}" for k in range(26)]
_INS = ["r_dense_features", "ids", *_TABLES, "W_top1", "b_top1", "W_top2", "b_top2", "W_top3"]


def kernel(**inputs):
    import numpy as _np
    import concourse.bacc as _bacc
    from concourse.bass_utils import run_bass_kernel_spmd as _run

    nc = _bacc.Bacc("TRN2", target_bir_lowering=False, num_devices=1)
    arrays, aps = {}, {}
    for name in _INS:
        a = _np.ascontiguousarray(inputs[name])
        arrays[f"in_{name}"] = a
        aps[name] = nc.dram_tensor(f"in_{name}", a.shape, mybir.dt.from_np(a.dtype), kind="ExternalInput").ap()
    batch = aps["ids"].shape[0]
    y = nc.dram_tensor("out_y", (batch, 1), F32, kind="ExternalOutput").ap()
    dlrm_program(nc, aps["r_dense_features"], aps["ids"], [aps[n] for n in _TABLES], aps["W_top1"],
                 aps["b_top1"], aps["W_top2"], aps["b_top2"], aps["W_top3"], y)
    r = _run(nc, [arrays], core_ids=[0])
    return r.results[0]["out_y"]
```

```python
import concourse.bass as bass
from concourse import mybir
from concourse.alu_op_type import AluOpType as ALU
from contextlib import ExitStack

F32 = mybir.dt.float32
F32R = mybir.dt.float32r
F16 = mybir.dt.float16
I32 = mybir.dt.int32
ACT = mybir.ActivationFunctionType

P = 128


def dlrm_program(nc, dense, ids, tables, w1, b1, w2, b2, w3, y_out):
    B, D = dense.shape
    NTAB = len(tables)
    F = NTAB + 1
    O1, O2 = w2.shape
    PAIRS = F * (F - 1) // 2
    TILES = B // P
    OC1, OC2 = O1 // P, O2 // P
    assert D == P and F == 27 and w1.shape[0] == D + PAIRS + D

    ROWS = 32
    QUADS = P // ROWS
    MOV = F - 1
    CHUNKS = MOV // QUADS
    DUP = MOV - CHUNKS * QUADS
    FIRST_MAIN = DUP + 1
    assert DUP + F <= ROWS

    SHARED = 18
    ONE_HOT = sorted(range(SHARED + 1, NTAB), key=lambda k: tables[k].shape[0]) + [SHARED]
    GATHERED = list(range(SHARED + 1))
    NOH = len(ONE_HOT)
    SHARED_TILE = TILES // 2

    def looked_up_rows(n):
        return slice(SHARED_TILE * P if ONE_HOT[n] == SHARED else 0, B)

    TP = 125
    TC = [tables[k].shape[0] // TP for k in ONE_HOT]
    TC_MAX = max(TC)
    assert all(tables[k].shape[0] == TP * c for k, c in zip(ONE_HOT, TC))
    assert all(tables[k].shape[0] <= 2048 for k in ONE_HOT)
    OH_RING = 8
    HALVES = 2
    CHUNKS_BEFORE = [sum(TC[:n]) for n in range(NOH + 1)]

    GROUPS = [GATHERED[n:n + 4] for n in range(0, len(GATHERED), 4)]
    NG = len(GROUPS)

    def group(t, g):
        return [k for k in GROUPS[g] if k != SHARED or t < SHARED_TILE]

    FIRST_BETWEEN = NOH - NG - 1
    assert FIRST_BETWEEN >= 0

    BLOCK = 4
    BLOCKS_PER_BANK = 4
    GRAM_BANKS = 2
    GROUP_BLOCKS = BLOCKS_PER_BANK * GRAM_BANKS
    GROUP_ROWS = GROUP_BLOCKS * BLOCK
    GRAMS = P // GROUP_ROWS

    WIDE = 2 * P
    ROUND_ROWS = [(0, WIDE)] + [(b, b + P) for b in range(WIDE, B, P)]
    WIDE_TILES = WIDE // P
    SPLITS = {GRAMS - 1: (0, P)}
    for t in range(1, TILES):
        for first, m in ((0, 1), (2, 2), (3, 3)):
            SPLITS[GRAMS * t + m] = (t * P + first * GROUP_ROWS, t * P + (m + 1) * GROUP_ROWS)

    def pair_row(i, j):
        return D + i * F - i * (i + 1) // 2 + (j - i - 1)

    ctx = ExitStack()
    with ctx:
        def sb(name, shape, dt):
            return ctx.enter_context(nc.sbuf_tensor(name, shape, dt))

        def sem(name):
            return ctx.enter_context(nc.semaphore(name))

        et = sb("et", [P, B, ROWS], F32)
        xt = sb("xt", [P, B], F32)
        z = sb("z", [P, CHUNKS, B], F32)
        rows = sb("rows", [P, 2, len(GATHERED), D], F32)
        x_sb = sb("x_sb", [P, TILES, D], F32)
        ids_sb = sb("ids_sb", [P, TILES, NTAB], I32)
        ids16 = sb("ids16", [P, TILES, NOH], F16)
        ident = sb("ident", [P, P], F32)
        ident16 = sb("ident16", [P, P], F16)
        first_row = sb("first_row", [P, 3], F32)
        table_sb = sb("table_sb", [P, 3, TC_MAX, D], F32)
        hi_mem = sb("hi_mem", [P, 3 * TC_MAX * D], F32R)
        lo_mem = sb("lo_mem", [P, 3 * TC_MAX * D], F32R)
        table_hi = hi_mem[:].rearrange("p (n c d) -> p n c d", n=3, c=TC_MAX)
        table_lo = lo_mem[:].rearrange("p (n c d) -> p n c d", n=3, c=TC_MAX)
        w1_hi = hi_mem[:, 0:(CHUNKS + 1) * O1].rearrange("p (c o) -> p c o", o=O1)
        w1_lo = lo_mem[:, 0:(CHUNKS + 1) * O1].rearrange("p (c o) -> p c o", o=O1)
        offset16 = sb("offset16", [P, 2, B], F16)
        one_hot_mem = sb("one_hot_mem", [P, OH_RING * B], F32R)
        PARTS = (CHUNKS + 1) * WIDE + OC1 * WIDE + OC1 * O2
        low_mem = sb("low_mem", [P, PARTS], F32R)
        one_hot = one_hot_mem[:].rearrange("p (n b) -> p n b", n=OH_RING)

        def wide_parts(mem):
            at = [0, (CHUNKS + 1) * WIDE, OC1 * WIDE, OC1 * O2]
            ends = [sum(at[:n + 1]) for n in range(len(at))]
            return [mem[:, ends[n]:ends[n + 1]].rearrange("p (c b) -> p c b", b=w)
                    for n, w in enumerate((WIDE, WIDE, O2))]

        zx_hi, h1_hi, w2_hi = wide_parts(one_hot_mem)
        zx_lo, h1_lo, w2_lo = wide_parts(low_mem)
        w1_sb = sb("w1_sb", [P, CHUNKS + 1, O1], F32)
        w1_pairs = w1_sb[:, 0:CHUNKS, :]
        w1_dense_sum = w1_sb[:, CHUNKS, :]
        w2_sb = sb("w2_sb", [P, OC1, O2], F32)
        NVEC = OC1 + 2 * OC2
        vec_rows = sb("vec_rows", [NVEC, P], F32)
        vec = sb("vec", [P, NVEC], F32)
        h1_mem = sb("h1_mem", [P, OC1 * WIDE], F32)
        h2_mem = sb("h2_mem", [P, OC2 * WIDE], F32)
        w1_dense = h1_mem[:, 0:2 * O1].rearrange("p (n o) -> p n o", o=O1)
        raw1 = table_sb[:, :, 0:OC1, :].rearrange("p n o d -> p n (o d)")
        h1_wide = h1_mem[:].rearrange("p (o b) -> p o b", b=WIDE)
        h1 = h1_mem[:].rearrange("p (n o b) -> p n o b", n=2, b=P)
        y_sb = sb("y_sb", [1, B], F32)
        ps = ctx.enter_context(nc.psum_tensor("ps", [P, 8, 512], F32))

        def sum_bank(n):
            return ps[:, 2 * (n % 2), :]

        def spread_bank(n):
            return ps[:, 2 * (n % 2) + 1, :]

        def tr_bank(n):
            return ps[:, 4 + n % 2, :]

        def gram_bank(gi):
            return GRAM_BANKS * ((gi + NOH) % 2)

        HALF1 = OC1 // 2
        HALF1_COLS = HALF1 * P

        def part_cols(b, b_end):
            return slice(b % WIDE, b % WIDE + b_end - b)

        def raw1_ps(h):
            return ps[:, 6 + h, 0:HALF1_COLS]

        def l1_ps(o):
            at = HALF1_COLS + (P if o == 1 else 0)
            return ps[:, 7 if o == 2 else 6, at:at + P]

        def wide_ps(o):
            return ps[:, 6 + o % 2, 0:WIDE]

        def l2_ps(r, o):
            return wide_ps(o) if r == 0 else ps[:, 4 + o, 0:P]

        def l3_ps(r):
            return ps[0:1, 6, WIDE:2 * WIDE] if r == 0 else ps[0:1, gram_bank(GRAMS * TILES - 2), 0:P]

        def h2(r, o):
            n = WIDE if r == 0 else P
            first = (r % 2) * OC2 * P + o * n if r else o * n
            return h2_mem[:, first:first + n]

        assert OC2 == 2 and OC1 == 4
        vec_ps = ps[:, 7, 0:NVEC]

        ids_loaded, x_loaded, vec_loaded = sem("ids_loaded"), sem("x_loaded"), sem("vec_loaded")
        wd_loaded, w2_loaded, w1_loaded = sem("wd_loaded"), sem("w2_loaded"), sem("w1_loaded")
        table_loaded = [[sem(f"table_loaded{n}_{h}") for h in range(HALVES)] for n in range(NOH)]
        gathered = [[sem(f"gathered{t}_{g}") for g in range(NG)] for t in range(TILES)]
        y_stored = sem("y_stored")
        ident_zero, ident_ready, first_row_ready = sem("ident_zero"), sem("ident_ready"), sem("first_row_ready")
        w1_zeroed, w1_cleared, wd_ready, et_padded = sem("w1_zeroed"), sem("w1_cleared"), sem("wd_ready"), sem("et_padded")
        ids16_ready, ident16_ready = sem("ids16_ready"), sem("ident16_ready")
        spread_done, offset_ready = sem("spread_done"), sem("offset_ready")
        hi_ready, lo_ready = sem("hi_ready"), sem("lo_ready")
        one_hot_ready, one_hot_used = sem("one_hot_ready"), sem("one_hot_used")
        sum_moved = sem("sum_moved")
        tr_done, tr_moved_act, tr_moved_dve = sem("tr_done"), sem("tr_moved_act"), sem("tr_moved_dve")
        vec_done, vec_ready = sem("vec_done"), sem("vec_ready")
        gram_done = sem("gram_done")
        main_act, main_dve, z_act, z_dve = sem("main_act"), sem("main_dve"), sem("z_act"), sem("z_dve")
        raw1_done, raw1_act, raw1_dve = sem("raw1_done"), sem("raw1_act"), sem("raw1_dve")
        l1_done, h1_act, h1_dve = sem("l1_done"), sem("h1_act"), sem("h1_dve")
        x_hi, x_lo, w1_hi_ready, w1_lo_ready = sem("x_hi"), sem("x_lo"), sem("w1_hi_ready"), sem("w1_lo_ready")
        w2_hi_ready, w2_lo_ready, z_hi, z_lo = sem("w2_hi_ready"), sem("w2_lo_ready"), sem("z_hi"), sem("z_lo")
        wide1_done, wide1_relu, wide1_hi, wide1_lo = (sem(f"wide1_{x}") for x in ("done", "relu", "hi", "lo"))
        l2_done, h2_act, h2_dve = sem("l2_done"), sem("h2_act"), sem("h2_dve")
        l3_done, y_ready = sem("l3_done"), sem("y_ready")

        def tr_number(t, g):
            return 1 + t * NG + g

        def by_act(n):
            return n % 2 == 0 or n <= tr_number(1, NG - 1)

        def moved_by_act(n):
            return sum(by_act(m) for m in range(n + 1))

        def moved_by_dve(n):
            return n + 1 - moved_by_act(n)

        def ahead_in_gram(t, m):
            return {0: (1,), 1: (2,), 2: range(3, NG)}.get(m, ()) if t < WIDE_TILES - 1 else ()

        def ahead_in_layer1(t, o):
            if t + 1 == TILES:
                return ()
            if t < WIDE_TILES:
                return ((0, 1), (2,), (), (3,), range(4, NG))[o]
            return ((0, 1), (2,), (3,), range(4, NG))[o]

        W1_AHEAD = 2

        def between(n):
            i = n - FIRST_BETWEEN
            return [divmod(i, NG)] if i >= 0 else []

        def half(n, h):
            return slice(h * TC[n] // HALVES, (h + 1) * TC[n] // HALVES)

        def w1_pieces():
            for i in range(F - 1):
                skip = max(0, i + 1 - FIRST_MAIN)
                g, c = divmod(skip, CHUNKS)
                if c:
                    yield g, 1, DUP + i, c, CHUNKS - c, pair_row(i, FIRST_MAIN + skip)
                    g += 1
                if g < QUADS:
                    yield g, QUADS - g, DUP + i, 0, CHUNKS, pair_row(i, FIRST_MAIN + CHUNKS * g)
            for i in range(DUP):
                yield 0, 1, i, i, DUP - i, pair_row(i, i + 1)

        PIECES = list(w1_pieces())
        ZERO_CHUNKS = CHUNKS // 2
        SHARE = 4

        block = ctx.enter_context(nc.Block())

        @block.sync
        def _(sp):
            def load_table(n):
                if n >= 3:
                    sp.wait_ge(lo_ready, HALVES * (n - 2))
                src = tables[ONE_HOT[n]].rearrange("(p c) d -> p c d", p=TP)
                for h in range(HALVES):
                    sp.dma_start(table_sb[0:TP, n % 3, half(n, h), :], src[:, half(n, h), :])\
                      .then_inc(table_loaded[n][h], 16)

            def load_w1(pieces):
                for g, ng, p, c, nc_, row in pieces:
                    src = w1[row:row + ng * nc_, :].rearrange("(g c) o -> g c o", g=ng)
                    first = ROWS * g + p
                    dst = w1_pairs[first:first + ROWS * (ng - 1) + 1:ROWS, c:c + nc_, :]
                    sp.dma_start(dst, src).then_inc(w1_loaded, 16)

            sp.dma_start(ids_sb[:], ids.rearrange("(t p) k -> p t k", p=P)).then_inc(ids_loaded, 16)
            load_table(0)
            load_table(1)
            sp.dma_start(x_sb[:], dense.rearrange("(t p) d -> p t d", p=P)).then_inc(x_loaded, 16)
            load_table(2)
            sp.dma_start(vec_rows[0:OC1, :], b1.rearrange("(o p) -> o p", p=P)).then_inc(vec_loaded, 16)
            sp.dma_start(vec_rows[OC1:OC1 + OC2, :], b2.rearrange("(o p) -> o p", p=P)).then_inc(vec_loaded, 16)
            sp.dma_start(vec_rows[OC1 + OC2:NVEC, :],
                         w3.rearrange("(o p) u -> o (p u)", p=P)).then_inc(vec_loaded, 16)
            sp.wait_ge(w1_zeroed, 1)
            sp.wait_ge(w1_cleared, ZERO_CHUNKS)
            for n in range(3, NOH):
                load_table(n)
                load_w1(PIECES[(n - 3) * SHARE:(n - 2) * SHARE])
            load_w1(PIECES[(NOH - 3) * SHARE:])
            sp.dma_start(w1_dense[:, 0, :], w1[0:D, :]).then_inc(wd_loaded, 16)
            sp.dma_start(w1_dense[:, 1, :], w1[D + PAIRS:D + PAIRS + D, :]).then_inc(wd_loaded, 16)
            sp.dma_start(w2_sb[:], w2.rearrange("(k p) o -> p k o", p=P)).then_inc(w2_loaded, 16)
            sp.wait_ge(y_ready, len(ROUND_ROWS))
            sp.dma_start(y_out.rearrange("b u -> u b"), y_sb[:]).then_inc(y_stored, 16)
            sp.wait_ge(y_stored, 16)

        @block.gpsimd
        def _(pool):
            pool.memset(ident[:], 0.0).then_inc(ident_zero, 1)
            pool.wait_ge(ident_zero, 1)
            pool.affine_select(out=ident[:], in_=ident[:], compare_op=ALU.not_equal, fill=1.0, base=0,
                               pattern=[[-1, P]], channel_multiplier=1).then_inc(ident_ready, 1)
            for n, c in enumerate(sorted(set(TC))):
                pool.iota(first_row[:, n:n + 1], pattern=[[0, 1]], base=0, channel_multiplier=-c,
                          allow_small_or_imprecise_dtypes=True).then_inc(first_row_ready, 1)
            pool.wait_ge(ids_loaded, 16)
            for t in range(TILES):
                for g in range(NG):
                    if t >= 2:
                        pool.wait_ge(tr_done, tr_number(t - 2, g) + 1)
                    for k in group(t, g):
                        pool.indirect_dma_start(
                            rows[:, t % 2, GATHERED.index(k), :], None, tables[k],
                            bass.IndirectOffsetOnAxis(ids_sb[:, t, k:k + 1], 0),
                        ).then_inc(gathered[t][g], 16)

        def runs(t, g):
            features = [k + 1 for k in group(t, g)]
            start = 0
            for n in range(1, len(features) + 1):
                if n == len(features) or features[n] != features[n - 1] + 1:
                    yield features[start], features[n - 1] + 1, start, DUP + features[start]
                    start = n
            again = [f for f in features if f < DUP]
            if again:
                yield again[0], again[-1] + 1, features.index(again[0]), again[0]

        def move_transposed(copy, t, g):
            bank = tr_bank(tr_number(t, g))
            for f, f_end, place, col in runs(t, g):
                n = f_end - f
                last = copy(et[:, t * P:(t + 1) * P, col:col + n].rearrange("p b f -> p f b"),
                            bank[:, place * P:(place + n) * P].rearrange("p (f b) -> p f b", f=n))
            return last

        def products(gi, q, w, n):
            b = gram_bank(gi)
            width = BLOCK * MOV
            v = ps[ROWS * q:ROWS * (q + 1), b:b + GRAM_BANKS, 0:BLOCKS_PER_BANK * width]
            v = v.rearrange("p k (m w) -> p k m w", m=BLOCKS_PER_BANK)
            return v[:, :, :, MOV * q + w:MOV * q + w + n]

        def slots(gi, q, g, c, n):
            b0 = gi * GROUP_ROWS
            v = z[ROWS * g:ROWS * (g + 1), c:c + n, b0:b0 + GROUP_ROWS]
            v = v.rearrange("p c (k m q) -> p k m c q", k=GRAM_BANKS, m=BLOCKS_PER_BANK)
            return v[:, :, :, :, q]

        def move_products(eng, copy, gi, quads, main_sem, z_sem):
            for g in range(QUADS):
                for q in quads:
                    copy(slots(gi, q, g, 0, CHUNKS),
                         products(gi, q, FIRST_MAIN - 1 + CHUNKS * g, CHUNKS)).then_inc(main_sem, 1)
            eng.wait_ge(main_sem, len(quads) * (QUADS * gi + 1))
            for q in quads:
                last = copy(slots(gi, q, 0, 0, DUP)[0:DUP], products(gi, q, 0, DUP)[0:DUP])
            last.then_inc(z_sem, 1)

        @block.scalar
        def _(act):
            def copy(out, in_):
                return act.activation(out, in_, ACT.Copy)

            def high_half(n, h):
                act.wait_ge(table_loaded[n][h], 16)
                copy(table_hi[0:TP, n % 3, half(n, h), :],
                     table_sb[0:TP, n % 3, half(n, h), :]).then_inc(hi_ready, 1)

            def high_part(n):
                if n >= 3:
                    act.wait_ge(one_hot_used, CHUNKS_BEFORE[n - 2])
                for h in range(HALVES):
                    high_half(n, h)

            def offsets(n):
                act.wait_ge(spread_done, n + 1)
                if n >= 2:
                    act.wait_ge(one_hot_ready, CHUNKS_BEFORE[n - 1])
                which = sorted(set(TC)).index(TC[n])
                rows_ = looked_up_rows(n)
                act.activation(offset16[0:TP, n % 2, rows_], spread_bank(n)[0:TP, rows_], ACT.Identity,
                               bias=first_row[0:TP, which:which + 1]).then_inc(offset_ready, 1)

            def move_sum(n):
                act.wait_ge(one_hot_used, CHUNKS_BEFORE[n + 1])
                col = DUP + ONE_HOT[n] + 1
                copy(et[:, looked_up_rows(n), col], sum_bank(n)[:, looked_up_rows(n)]).then_inc(sum_moved, 1)

            def move_group(t, g):
                n = tr_number(t, g)
                if by_act(n):
                    act.wait_ge(tr_done, n + 1)
                    move_transposed(copy, t, g).then_inc(tr_moved_act, 1)

            def relu1(t, parts):
                r = t - WIDE_TILES
                act.wait_ge(l1_done, 2 * r + (1 if parts[0] == 0 else 2))
                for o in parts:
                    last = act.activation(h1[:, t % 2, o, :], l1_ps(o), ACT.Relu, bias=vec[:, o:o + 1])
                last.then_inc(h1_act, 1)

            def relu2(r):
                act.wait_ge(l2_done, 2 * r + 1)
                act.activation(h2(r, 0), l2_ps(r, 0), ACT.Relu, bias=vec[:, OC1:OC1 + 1]).then_inc(h2_act, 1)

            def move_y(r):
                act.wait_ge(l3_done, r + 1)
                first, end = ROUND_ROWS[r]
                copy(y_sb[:, first:end], l3_ps(r)).then_inc(y_ready, 1)

            def w1_high(o):
                cols = slice(o * P, (o + 1) * P)
                copy(w1_hi[:, :, cols], w1_sb[:, :, cols]).then_inc(w1_hi_ready, 1)

            def z_high(gi):
                act.wait_ge(z_act, gi + 1)
                act.wait_ge(z_dve, gi + 1)
                copy(zx_hi[:, 0:CHUNKS, part_cols(*SPLITS[gi])], z[:, :, slice(*SPLITS[gi])]).then_inc(z_hi, 1)

            def x_high(b):
                copy(zx_hi[:, CHUNKS, :], xt[:, b:b + WIDE]).then_inc(x_hi, 1)

            def move_raw1(t):
                act.wait_ge(raw1_done, 2 * (t - WIDE_TILES) + 1)
                copy(raw1[:, t - WIDE_TILES, 0:HALF1_COLS], raw1_ps(0)).then_inc(raw1_act, 1)

            def wide_relu1(o):
                act.wait_ge(wide1_done, o + 1)
                act.activation(h1_wide[:, o, :], wide_ps(o), ACT.Relu, bias=vec[:, o:o + 1]).then_inc(wide1_relu, 1)
                act.wait_ge(wide1_relu, o + 1)
                copy(h1_hi[:, o, :], h1_wide[:, o, :]).then_inc(wide1_hi, 1)

            act.wait_ge(first_row_ready, len(set(TC)))
            copy(first_row[:, 2:3], first_row[:, 0:1])
            act.wait_ge(ident_ready, 1)
            act.activation(w1_pairs[:, ZERO_CHUNKS:, :].rearrange("p c (n o) -> p (c n) o", o=P),
                           ident[:, None, :].to_broadcast([P, (CHUNKS - ZERO_CHUNKS) * OC1, P]), ACT.Copy,
                           scale=0.0).then_inc(w1_zeroed, 1)
            high_half(0, 0)
            offsets(0)
            high_half(0, 1)
            high_part(1)
            offsets(1)
            high_part(2)
            act.wait_ge(tr_done, 1)
            copy(xt[:], tr_bank(0))
            copy(et[:, :, 0], tr_bank(0))
            copy(et[:, :, DUP], tr_bank(0)).then_inc(tr_moved_act, 1)
            act.wait_ge(vec_done, 1)
            copy(vec[:], vec_ps).then_inc(vec_ready, 1)
            for n in range(NOH):
                move_sum(n)
                for t, g in between(n):
                    move_group(t, g)
                if n + 2 < NOH:
                    offsets(n + 2)
                if n + 3 < NOH:
                    high_part(n + 3)
                if n == 0:
                    act.wait_ge(tr_moved_act, 1)
                    copy(et[:, :, DUP + F:ROWS].rearrange("p b f -> p f b"),
                         xt[:, None, :].to_broadcast([P, ROWS - DUP - F, B])).then_inc(et_padded, 1)

            def move_gram(t, m):
                gi = GRAMS * t + m
                act.wait_ge(gram_done, gi + 1)
                move_products(act, copy, gi, (2, 3), main_act, z_act)

            x_high(0)
            act.wait_ge(vec_ready, 1)
            act.wait_ge(w1_loaded, 16 * len(PIECES))
            act.wait_ge(wd_ready, 1)
            for m in range(GRAMS):
                move_gram(0, m)
                for g in ahead_in_gram(0, m):
                    move_group(1, g)
                if m < W1_AHEAD:
                    w1_high(m)
            z_high(GRAMS - 1)
            for m in range(GRAMS):
                move_gram(1, m)
                if GRAMS + m in SPLITS:
                    z_high(GRAMS + m)
            for o in range(OC1 + 1):
                for g in ahead_in_layer1(WIDE_TILES - 1, o):
                    move_group(WIDE_TILES, g)
                if o == 0:
                    for part in range(W1_AHEAD, OC1):
                        w1_high(part)
                if o == 2:
                    act.wait_ge(w2_loaded, 16)
                    copy(w2_hi, w2_sb[:]).then_inc(w2_hi_ready, 1)
                if o < OC1:
                    wide_relu1(o)
            x_high(WIDE)
            for t in range(WIDE_TILES, TILES):
                r = t - WIDE_TILES
                if r == 0:
                    relu2(0)
                for m in range(GRAMS):
                    move_gram(t, m)
                    if r == 0 and m == 0:
                        move_y(0)
                    if t > WIDE_TILES and m == 0:
                        relu1(t - 1, (3,))
                    if m == GRAMS - 1:
                        for g in ahead_in_layer1(t, 0)[:1]:
                            move_group(t + 1, g)
                    if GRAMS * t + m in SPLITS:
                        z_high(GRAMS * t + m)
                if r >= 1:
                    relu2(r)
                for g in (*ahead_in_layer1(t, 0)[1:], *ahead_in_layer1(t, 1)):
                    move_group(t + 1, g)
                move_raw1(t)
                if r >= 1:
                    move_y(r)
                for g in ahead_in_layer1(t, 2):
                    move_group(t + 1, g)
                relu1(t, (0, 1))
                for g in ahead_in_layer1(t, 3):
                    move_group(t + 1, g)
            relu1(TILES - 1, (3,))
            relu2(TILES - WIDE_TILES)
            move_y(TILES - WIDE_TILES)

        @block.vector
        def _(dve):
            def copy(out, in_):
                return dve.tensor_copy(out, in_)

            def low_part(n):
                if n >= 3:
                    dve.wait_ge(one_hot_used, CHUNKS_BEFORE[n - 2])
                for h in range(HALVES):
                    low_half(n, h)

            def low_half(n, h):
                dve.wait_ge(hi_ready, HALVES * n + h + 1)
                dve.tensor_tensor(table_lo[0:TP, n % 3, half(n, h), :], table_sb[0:TP, n % 3, half(n, h), :],
                                  table_hi[0:TP, n % 3, half(n, h), :], ALU.subtract).then_inc(lo_ready, 1)

            def one_hots(n, chunks):
                dve.wait_ge(offset_ready, n + 1)
                for c in chunks:
                    m = CHUNKS_BEFORE[n] + c
                    if m >= OH_RING:
                        dve.wait_ge(one_hot_used, m - OH_RING + 1)
                    rows_ = looked_up_rows(n)
                    dve.tensor_scalar(one_hot[0:TP, m % OH_RING, rows_], offset16[0:TP, n % 2, rows_], float(c), None,
                                      ALU.is_equal).then_inc(one_hot_ready, 1)

            def move_group(t, g):
                n = tr_number(t, g)
                if not by_act(n):
                    dve.wait_ge(tr_done, n + 1)
                    move_transposed(copy, t, g).then_inc(tr_moved_dve, 1)

            def relu1(t):
                dve.wait_ge(l1_done, 2 * (t - WIDE_TILES) + 2)
                dve.tensor_scalar(h1[:, t % 2, 2, :], l1_ps(2), vec[:, 2:3], 0.0,
                                  ALU.add, ALU.max).then_inc(h1_dve, 1)

            def relu2(r):
                dve.wait_ge(l2_done, 2 * r + 2)
                dve.tensor_scalar(h2(r, 1), l2_ps(r, 1), vec[:, OC1 + 1:OC1 + 2], 0.0,
                                  ALU.add, ALU.max).then_inc(h2_dve, 1)

            def w1_low(o):
                dve.wait_ge(w1_hi_ready, o + 1)
                cols = slice(o * P, (o + 1) * P)
                dve.tensor_tensor(w1_lo[:, :, cols], w1_sb[:, :, cols], w1_hi[:, :, cols],
                                  ALU.subtract).then_inc(w1_lo_ready, 1)

            def z_low(gi):
                dve.wait_ge(z_hi, sorted(SPLITS).index(gi) + 1)
                cols = part_cols(*SPLITS[gi])
                dve.tensor_tensor(zx_lo[:, 0:CHUNKS, cols], z[:, :, slice(*SPLITS[gi])],
                                  zx_hi[:, 0:CHUNKS, cols], ALU.subtract).then_inc(z_lo, 1)

            def lows_behind(gi):
                def at_once(n):
                    return n % GRAMS == GRAMS - 1 and n >= GRAMS
                if gi - 1 in SPLITS and not at_once(gi - 1):
                    z_low(gi - 1)
                if gi in SPLITS and at_once(gi):
                    z_low(gi)

            def x_low(b):
                dve.wait_ge(x_hi, b // WIDE + 1)
                dve.tensor_tensor(zx_lo[:, CHUNKS, :], xt[:, b:b + WIDE], zx_hi[:, CHUNKS, :],
                                  ALU.subtract).then_inc(x_lo, 1)

            def move_raw1(t):
                dve.wait_ge(raw1_done, 2 * (t - WIDE_TILES) + 2)
                copy(raw1[:, t - WIDE_TILES, HALF1_COLS:O1], raw1_ps(1)).then_inc(raw1_dve, 1)

            def wide_low1(o):
                dve.wait_ge(wide1_hi, o + 1)
                dve.tensor_tensor(h1_lo[:, o, :], h1_wide[:, o, :], h1_hi[:, o, :],
                                  ALU.subtract).then_inc(wide1_lo, 1)

            dve.wait_ge(ident_ready, 1)
            copy(ident16[:], ident[:]).then_inc(ident16_ready, 1)
            dve.memset(w1_pairs[:, 0, :], 0.0).then_inc(w1_cleared, 1)
            dve.memset(w1_pairs[:, 1, :], 0.0).then_inc(w1_cleared, 1)
            dve.wait_ge(ids_loaded, 16)
            copy(ids16[:], ids_sb[:, :, SHARED:]).then_inc(ids16_ready, 1)
            for c in range(2, ZERO_CHUNKS):
                dve.memset(w1_pairs[:, c, :], 0.0).then_inc(w1_cleared, 1)
            for n in range(NOH):
                if n == 0:
                    for h in range(HALVES):
                        low_half(n, h)
                        one_hots(n, range(TC[n])[half(n, h)])
                else:
                    low_part(n)
                    one_hots(n, range(TC[n]))
                for t, g in between(n - 1):
                    move_group(t, g)
            for t, g in between(NOH - 1):
                move_group(t, g)

            def move_gram(t, m):
                gi = GRAMS * t + m
                dve.wait_ge(gram_done, gi + 1)
                move_products(dve, copy, gi, (0, 1), main_dve, z_dve)

            dve.wait_ge(wd_loaded, 32)
            dve.tensor_tensor(w1_dense_sum, w1_dense[:, 0, :], w1_dense[:, 1, :], ALU.add).then_inc(wd_ready, 1)
            x_low(0)
            dve.wait_ge(vec_ready, 1)
            for m in range(GRAMS):
                move_gram(0, m)
                for g in ahead_in_gram(0, m):
                    move_group(1, g)
                if 1 <= m <= W1_AHEAD:
                    w1_low(m - 1)
            for m in range(GRAMS):
                move_gram(1, m)
                lows_behind(GRAMS + m)
            for o in range(OC1 + 1):
                for g in ahead_in_layer1(WIDE_TILES - 1, o):
                    move_group(WIDE_TILES, g)
                if W1_AHEAD + o < OC1:
                    w1_low(W1_AHEAD + o)
                if W1_AHEAD + o == OC1:
                    dve.wait_ge(w2_hi_ready, 1)
                    dve.tensor_tensor(w2_lo, w2_sb[:], w2_hi, ALU.subtract).then_inc(w2_lo_ready, 1)
                if o < OC1:
                    wide_low1(o)
            x_low(WIDE)
            for t in range(WIDE_TILES, TILES):
                r = t - WIDE_TILES
                if r == 0:
                    relu2(0)
                for m in range(GRAMS):
                    move_gram(t, m)
                    if t > WIDE_TILES and m == 0:
                        relu1(t - 1)
                    lows_behind(GRAMS * t + m)
                if r >= 1:
                    relu2(r)
                for step in range(4):
                    for g in ahead_in_layer1(t, step):
                        move_group(t + 1, g)
                move_raw1(t)
            relu1(TILES - 1)
            relu2(TILES - WIDE_TILES)

        @block.tensor
        def _(pe):
            def spread(n):
                if n >= 2:
                    pe.wait_ge(offset_ready, n - 1)
                at = ONE_HOT[n] - SHARED
                for t in range(looked_up_rows(n).start // P, TILES):
                    last = pe.matmul(spread_bank(n)[:, t * P:(t + 1) * P],
                                     ids16[:, t, at:at + 1].to_broadcast([P, P]), ident16[:],
                                     start=True, stop=True)
                last.then_inc(spread_done, 1)

            def look_up(n):
                if n >= 2:
                    pe.wait_ge(sum_moved, n - 1)
                rows_ = looked_up_rows(n)
                for c in range(TC[n]):
                    m = CHUNKS_BEFORE[n] + c
                    for h in range(HALVES):
                        if c == half(n, h).start:
                            pe.wait_ge(lo_ready, HALVES * n + h + 1)
                    pe.wait_ge(one_hot_ready, m + 1)
                    pe.matmul(sum_bank(n)[:, rows_], table_hi[0:TP, n % 3, c, :], one_hot[0:TP, m % OH_RING, rows_],
                              start=c == 0, stop=False)
                    last = pe.matmul(sum_bank(n)[:, rows_], table_lo[0:TP, n % 3, c, :], one_hot[0:TP, m % OH_RING, rows_],
                                     start=False, stop=c == TC[n] - 1)
                    last.then_inc(one_hot_used, 1)

            def transposes(t, g):
                n = tr_number(t, g)
                pe.wait_ge(gathered[t][g], 16 * len(group(t, g)))
                if n >= 2:
                    if by_act(n - 2):
                        pe.wait_ge(tr_moved_act, moved_by_act(n - 2))
                    else:
                        pe.wait_ge(tr_moved_dve, moved_by_dve(n - 2))
                for place, k in enumerate(group(t, g)):
                    last = pe.transpose(tr_bank(n)[:, place * P:(place + 1) * P],
                                        rows[:, t % 2, GATHERED.index(k), :], ident[:])
                last.then_inc(tr_done, 1)

            def features_ready(t):
                if t == 0:
                    pe.wait_ge(et_padded, 1)
                    pe.wait_ge(sum_moved, NOH - 1)
                pe.wait_ge(tr_moved_act, moved_by_act(tr_number(t, NG - 1)))
                if t >= 2:
                    pe.wait_ge(tr_moved_dve, moved_by_dve(tr_number(t, NG - 1)))

            def gram(gi):
                if gi == 1:
                    pe.wait_ge(sum_moved, NOH)
                if gi >= 2:
                    pe.wait_ge(z_act, gi - 1)
                    pe.wait_ge(z_dve, gi - 1)
                for m in range(GROUP_BLOCKS):
                    b0 = gi * GROUP_ROWS + m * BLOCK
                    bank, at = divmod(m, BLOCKS_PER_BANK)
                    out = ps[:, gram_bank(gi) + bank, at * BLOCK * MOV:(at + 1) * BLOCK * MOV]
                    last = pe.matmul(out, et[:, b0:b0 + BLOCK, 0:ROWS], et[:, b0:b0 + BLOCK, DUP + 1:DUP + F],
                                     start=True, stop=True)
                last.then_inc(gram_done, 1)

            def parts_product(out, w_hi, w_lo, x_hi_, x_lo_, start, stop):
                pe.matmul(out, w_hi, x_lo_, start=start, stop=False)
                pe.matmul(out, w_lo, x_hi_, start=False, stop=False)
                return pe.matmul(out, w_hi, x_hi_, start=False, stop=stop)

            def half_product(t, h, c, start, stop):
                rows_ = part_cols(t * P, (t + 1) * P)
                cols = slice(h * HALF1_COLS, (h + 1) * HALF1_COLS)
                return parts_product(raw1_ps(h), zx_hi[:, c, rows_], zx_lo[:, c, rows_], w1_hi[:, c, cols],
                                     w1_lo[:, c, cols], start, stop)

            def layer1_dense(t):
                if t == WIDE_TILES:
                    pe.wait_ge(y_ready, 1)
                    pe.wait_ge(h2_dve, 1)
                else:
                    pe.wait_ge(h1_act, 2 * (t - WIDE_TILES))
                    pe.wait_ge(h1_dve, t - WIDE_TILES)
                pe.wait_ge(x_lo, t // WIDE_TILES + 1)
                half_product(t, 0, CHUNKS, True, False)
                half_product(t, 1, CHUNKS, True, False)

            def layer1(t, h):
                pe.wait_ge(z_lo, sum(gi < GRAMS * (t + 1) for gi in SPLITS))
                for c in range(CHUNKS):
                    if h == 1 and c == CHUNKS // 2:
                        layer1_transposes(t, 0)
                    if h == 1 and c == CHUNKS - 1:
                        for g in ahead_in_layer1(t, 3):
                            transposes(t + 1, g)
                    last = half_product(t, h, c, False, c == CHUNKS - 1)
                last.then_inc(raw1_done, 1)

            def layer1_transposes(t, h):
                pe.wait_ge(raw1_dve if h else raw1_act, t - WIDE_TILES + 1)
                if h:
                    pe.wait_ge(h1_act, 2 * (t - WIDE_TILES) + 1)
                for o in range(h * HALF1, (h + 1) * HALF1):
                    last = pe.transpose(l1_ps(o), raw1[:, t - WIDE_TILES, o * P:(o + 1) * P], ident[:])
                last.then_inc(l1_done, 1)

            def wide_product(o, c, start, stop):
                cols = slice(o * P, (o + 1) * P)
                return parts_product(wide_ps(o), w1_hi[:, c, cols], w1_lo[:, c, cols], zx_hi[:, c, :],
                                     zx_lo[:, c, :], start, stop)

            def wide_dense(o):
                if o == 0:
                    pe.wait_ge(vec_ready, 1)
                    pe.wait_ge(x_lo, 1)
                if o >= 2:
                    pe.wait_ge(wide1_relu, o - 1)
                pe.wait_ge(w1_lo_ready, o + 1)
                wide_product(o, CHUNKS, True, False)

            def wide_layer1(o):
                if o == 0:
                    wide_dense(0)
                    wide_dense(1)
                    pe.wait_ge(z_lo, sum(gi < GRAMS * WIDE_TILES for gi in SPLITS))
                if o >= 2:
                    wide_dense(o)
                for c in range(CHUNKS):
                    last = wide_product(o, c, False, c == CHUNKS - 1)
                last.then_inc(wide1_done, 1)

            def wide_layer2():
                pe.wait_ge(w2_lo_ready, 1)
                for ks in (range(OC1 - 1), (OC1 - 1,)):
                    for o in range(OC2):
                        cols = slice(o * P, (o + 1) * P)
                        pe.wait_ge(wide1_relu, OC1 - 1 + o)
                        for k in ks:
                            pe.wait_ge(wide1_lo, k + 1)
                            last = parts_product(wide_ps(o), w2_hi[:, k, cols], w2_lo[:, k, cols],
                                                 h1_hi[:, k, :], h1_lo[:, k, :], k == 0, k == OC1 - 1)
                        if k == OC1 - 1:
                            last.then_inc(l2_done, 1)

            def layer2_product(t, o, k):
                return pe.matmul(l2_ps(t - WIDE_TILES + 1, o), w2_sb[:, k, o * P:(o + 1) * P], h1[:, t % 2, k, :],
                                 start=k == 0, stop=k == OC1 - 1)

            def layer2(t):
                r = t - WIDE_TILES + 1
                if r >= 2:
                    pe.wait_ge(h2_act, r)
                    pe.wait_ge(h2_dve, r)
                pe.wait_ge(tr_moved_act, moved_by_act(tr_number(TILES - 1, NG - 1)))
                pe.wait_ge(tr_moved_dve, moved_by_dve(tr_number(TILES - 1, NG - 1)))
                pe.wait_ge(h1_act, 2 * r - 1)
                for o in range(OC2):
                    for k in range(HALF1):
                        layer2_product(t, o, k)
                    if o == 0 and t == TILES - 1:
                        layer1_transposes(t, 1)
                for o in range(OC2):
                    pe.wait_ge(h1_dve, r)
                    layer2_product(t, o, 2)
                    pe.wait_ge(h1_act, 2 * r)
                    layer2_product(t, o, 3).then_inc(l2_done, 1)

            def layer3(r):
                if r >= 1:
                    pe.wait_ge(z_act, GRAMS * TILES - 1)
                    pe.wait_ge(z_dve, GRAMS * TILES - 1)
                    pe.wait_ge(y_ready, r)
                pe.wait_ge(h2_act, r + 1)
                for k in range(OC2):
                    if k == 1:
                        pe.wait_ge(h2_dve, r + 1)
                    last = pe.matmul(l3_ps(r), vec[:, OC1 + OC2 + k:OC1 + OC2 + k + 1], h2(r, k),
                                     start=k == 0, stop=k == OC2 - 1)
                last.then_inc(l3_done, 1)

            def small_transposes():
                pe.wait_ge(ident_ready, 1)
                pe.wait_ge(x_loaded, 16)
                for t in range(TILES):
                    last = pe.transpose(tr_bank(0)[:, t * P:(t + 1) * P], x_sb[:, t, :], ident[:])
                last.then_inc(tr_done, 1)
                pe.wait_ge(vec_loaded, 48)
                pe.transpose(vec_ps, vec_rows[:], ident[0:NVEC, 0:NVEC]).then_inc(vec_done, 1)

            def warm_up(n):
                for _ in range(n):
                    pe.matmul(ps[:, 6, 0:P], ident16[:], ident16[:], start=True, stop=True)

            pe.wait_ge(ident16_ready, 1)
            warm_up(14)
            pe.wait_ge(ids16_ready, 1)
            spread(0)
            spread(1)
            warm_up(13)
            for n in range(NOH):
                look_up(n)
                if n == 0:
                    small_transposes()
                if n + 2 < NOH:
                    spread(n + 2)
                for t, g in between(n):
                    transposes(t, g)
            for t in range(WIDE_TILES):
                features_ready(t)
                for m in range(GRAMS):
                    gram(GRAMS * t + m)
                    for g in ahead_in_gram(t, m):
                        transposes(t + 1, g)
            for o in range(OC1 + 1):
                for g in ahead_in_layer1(WIDE_TILES - 1, o):
                    transposes(WIDE_TILES, g)
                if o < OC1:
                    wide_layer1(o)
            wide_layer2()
            for t in range(WIDE_TILES, TILES):
                features_ready(t)
                for m in range(GRAMS):
                    gram(GRAMS * t + m)
                    if t == WIDE_TILES and m == 0:
                        layer3(0)
                    if t > WIDE_TILES and m == 0:
                        layer1_transposes(t - 1, 1)
                if t > WIDE_TILES:
                    layer2(t - 1)
                for g in ahead_in_layer1(t, 0):
                    transposes(t + 1, g)
                layer1_dense(t)
                for h in range(2):
                    for g in ahead_in_layer1(t, h + 1):
                        transposes(t + 1, g)
                    layer1(t, h)
                    if h == 0 and t > WIDE_TILES:
                        layer3(t - WIDE_TILES)
            layer2(TILES - 1)
            layer3(TILES - WIDE_TILES)


_TABLES = [f"tbl_{k}" for k in range(26)]
_INS = ["r_dense_features", "ids", *_TABLES, "W_top1", "b_top1", "W_top2", "b_top2", "W_top3"]


def kernel(**inputs):
    import numpy as _np
    import concourse.bacc as _bacc
    from concourse.bass_utils import run_bass_kernel_spmd as _run

    nc = _bacc.Bacc("TRN2", target_bir_lowering=False, num_devices=1)
    arrays, aps = {}, {}
    for name in _INS:
        a = _np.ascontiguousarray(inputs[name])
        arrays[f"in_{name}"] = a
        aps[name] = nc.dram_tensor(f"in_{name}", a.shape, mybir.dt.from_np(a.dtype), kind="ExternalInput").ap()
    batch = aps["ids"].shape[0]
    y = nc.dram_tensor("out_y", (batch, 1), F32, kind="ExternalOutput").ap()
    dlrm_program(nc, aps["r_dense_features"], aps["ids"], [aps[n] for n in _TABLES], aps["W_top1"],
                 aps["b_top1"], aps["W_top2"], aps["b_top2"], aps["W_top3"], y)
    r = _run(nc, [arrays], core_ids=[0])
    return r.results[0]["out_y"]
```
